# Optimizing a Trainium2 kernel written in Bass

```python
import numpy as np
import jax
import jax.numpy as jnp

def _softmax(x, axis=-1):
    return jax.nn.softmax(x, axis=axis)

def _gelu(x):
    return jax.nn.gelu(x, approximate=True)

def _silu(x):
    return jax.nn.silu(x)

def _sigmoid(x):
    return jax.nn.sigmoid(x)

def _layernorm(x, axis=-1, eps=1e-05):
    m = jnp.mean(x, axis=axis, keepdims=True)
    v = jnp.var(x, axis=axis, keepdims=True)
    return (x - m) / jnp.sqrt(v + eps)

def _scatter_add(tgt, idx, src, axis=0):
    return tgt.at[idx].add(src)

def _segment_sum(src, seg, n):
    return jax.ops.segment_sum(src, seg, n)
kernel_name = 'mk_seq_preln_d1_jaxref_r2_5c68e9'

def setup_inputs(seed: int=0):
    np.random.seed(seed)
    _w = jnp.asarray

    def _L0_attn_setup():
        import jax, jax.numpy as jnp
        import numpy as np
        import math
        B, N, E, D = (4, 4096, 512, 64)
        key = jax.random.key(seed)
        kx, kq, kk, kv, ko = jax.random.split(key, 5)
        x = jax.random.normal(kx, (B, N, E), dtype=jnp.float32)
        wq = jnp.sign(jax.random.normal(kq, (D, E), dtype=jnp.float32)) / math.sqrt(E)
        wk = jnp.sign(jax.random.normal(kk, (D, E), dtype=jnp.float32)) / math.sqrt(E)
        wv = jnp.sign(jax.random.normal(kv, (D, E), dtype=jnp.float32)) / math.sqrt(E)
        wo = jnp.sign(jax.random.normal(ko, (E, D), dtype=jnp.float32)) / math.sqrt(D)
        return {'x': x, 'wq': wq, 'wk': wk, 'wv': wv, 'wo': wo}
    _L0_attn_in = _L0_attn_setup()

    def _L0_ffn_setup():
        import jax, jax.numpy as jnp
        import numpy as np
        EPS = 1e-06
        SINKHORN_ITERS = 8

        def _sinkhorn(logits, num_iters=SINKHORN_ITERS, eps=EPS):
            t = jnp.log(jnp.clip(logits, eps, None))
            for _ in range(num_iters):
                t = t - jax.nn.logsumexp(t, axis=-2, keepdims=True)
                t = t - jax.nn.logsumexp(t, axis=-1, keepdims=True)
            return jnp.exp(t)
        key = jax.random.key(seed)
        k1, k2, k3 = jax.random.split(key, 3)
        b, n, d, e, h = (4, 2048, 512, 8, 1)
        x = jax.random.normal(k1, (b, n, d), dtype=jnp.float32)
        gate_w = jax.random.normal(k2, (h, d, e), dtype=jnp.float32) * d ** (-0.5)
        experts = jax.random.normal(k3, (e, d, d), dtype=jnp.float32) * d ** (-0.5)
        return {'x': x, 'gate_w': gate_w, 'experts': experts}
    _L0_ffn_in = _L0_ffn_setup()
    _d = {'L0_attn_x': _L0_attn_in['x'], 'L0_attn_wq': _L0_attn_in['wq'], 'L0_attn_wk': _L0_attn_in['wk'], 'L0_attn_wv': _L0_attn_in['wv'], 'L0_attn_wo': _L0_attn_in['wo'], 'L0_ffn_gate_w': _L0_ffn_in['gate_w'], 'L0_ffn_experts': _L0_ffn_in['experts']}
    _x0 = _d['L0_attn_x']
    _d['L0_attn_x'] = jax.random.normal(jax.random.fold_in(jax.random.key(seed), 1), (8, 4096, 512), dtype=_x0.dtype)
    del _x0
    return _d

def reference(L0_attn_x, L0_attn_wq, L0_attn_wk, L0_attn_wv, L0_attn_wo, L0_ffn_gate_w, L0_ffn_experts):

    def _L0_attn_ref(x, wq, wk, wv, wo):
        import jax, jax.numpy as jnp
        import numpy as np
        import math
        B, N, E, D = (4, 4096, 512, 64)
        Q = jnp.einsum('bne,de->bnd', x, wq)
        K = jnp.einsum('bne,de->bnd', x, wk)
        V = jnp.einsum('bne,de->bnd', x, wv)
        energy = jnp.einsum('bnd,bne->bde', K, V)
        context = jnp.einsum('bnd,bde->bne', Q, energy)
        context = context * jnp.asarray(math.sqrt(3.0 / D), dtype=context.dtype)
        out = jnp.einsum('bnd,ed->bne', context, wo)
        return out

    def _L0_ffn_ref(x, gate_w, experts):
        import jax, jax.numpy as jnp
        import numpy as np
        EPS = 1e-06
        SINKHORN_ITERS = 8

        def _sinkhorn(logits, num_iters=SINKHORN_ITERS, eps=EPS):
            t = jnp.log(jnp.clip(logits, eps, None))
            for _ in range(num_iters):
                t = t - jax.nn.logsumexp(t, axis=-2, keepdims=True)
                t = t - jax.nn.logsumexp(t, axis=-1, keepdims=True)
            return jnp.exp(t)
        b, n, d = x.shape
        e = experts.shape[0]
        m = n // e
        xh = x[:, None]
        gate_logits = jnp.einsum('bhnd,hde->bhne', xh, gate_w)
        gates = _sinkhorn(gate_logits)
        gates_t = jnp.swapaxes(gates, -2, -1)
        gate_values, routed_idx = jax.lax.top_k(gates_t, m)
        hard = (gate_values > 0.5).astype(x.dtype)
        gate_values = hard + gate_values - jax.lax.stop_gradient(gate_values)
        routed = jnp.take_along_axis(xh[:, :, None], routed_idx[..., None], axis=3)
        out_e = jnp.einsum('bhemi,eio->bhemo', routed, experts)
        out_e = out_e * gate_values[..., None]
        out = jnp.zeros_like(xh)
        bi = jnp.arange(b)[:, None, None, None]
        hi = jnp.arange(1)[None, :, None, None]
        out = out.at[bi, hi, routed_idx].set(out_e)
        return out[:, 0]
    x = L0_attn_x
    x = x + _L0_attn_ref(_layernorm(x, axis=-1), L0_attn_wq, L0_attn_wk, L0_attn_wv, L0_attn_wo)
    x = x + _L0_ffn_ref(_layernorm(x, axis=-1), L0_ffn_gate_w, L0_ffn_experts)
    return x

_drawn_inputs = setup_inputs


def setup_inputs(seed=0):
    import zlib

    import numpy as np

    out = dict(_drawn_inputs(seed))
    spreads = {}
    factors = {'L0_ffn_gate_w': 32.529, 'L0_ffn_experts': 31.91}
    for name, (base, spread) in spreads.items():
        noise = np.random.default_rng([zlib.crc32(name.encode()), seed]).standard_normal(out[name].shape)
        drawn = base * np.exp(spread * noise) if base else spread * noise
        out[name] = jnp.asarray(drawn.astype(out[name].dtype))
    for name, factor in factors.items():
        out[name] = (out[name] * factor).astype(out[name].dtype)
    return out
```

```python
from contextlib import ExitStack


def linear_attention_moe_kernel(nc, x, wq, wk, wv, wo, gate_w, experts, out):
    import concourse.bass as bass
    from concourse import mybir

    F32, F16, I32 = mybir.dt.float32, mybir.dt.float16, mybir.dt.int32
    ALU, ACT, AX = mybir.AluOpType, mybir.ActivationFunctionType, mybir.AxisListType

    P = 128
    B, N, E = x.shape
    D = wq.shape[0]
    X = experts.shape[0]
    CH = E // P
    TB = N // P
    K = B * TB
    GT = 4
    GB = TB // GT
    NG = B * GB
    RING = GB + 4
    CAP = N // X
    LN_EPS, CLIP_EPS, ITERS = 1e-5, 1e-6, 8
    OUT_SCALE = (3.0 / D) ** 0.5

    SY, SW, SQ, SGATE, SLOG, SX = 64.0, 256.0, 64.0, 16.0, 1.0 / 16, 16.0
    NC = 3 * D + X
    TILES = -(-(K + X) // 4) * 4
    TABLE = TILES + 4
    HALF = TABLE
    EMPTY = float(1 << 20)

    ctx = ExitStack()
    with ctx:
        def sb(name, shape, dt):
            return ctx.enter_context(nc.sbuf_tensor(name, shape, dt))

        def pb(name, shape, dt):
            return ctx.enter_context(nc.psum_tensor(name, shape, dt))

        def sem(name):
            return ctx.enter_context(nc.semaphore(name))

        big = sb("big", [P, RING * GT * E], F32)
        xr = big[:, :].rearrange("p (l t e) -> p l t e", l=RING, t=GT)
        HE = X * CH * E // 2
        e_hi = big[:, 0:HE].bitcast(F16).rearrange("p (x c n) -> p x c n", x=X, c=CH)
        e_lo = big[:, HE:2 * HE].bitcast(F16).rearrange("p (x c n) -> p x c n", x=X, c=CH)
        half = 2 * HE
        e_f = big[:, half:half + HE].rearrange("p (x c n) -> p x c n", x=X // 2, c=CH)
        xg = big[:, half:half + 4 * E].rearrange("p (i e) -> p i e", i=4)
        yo = big[:, half + 4 * E:half + 8 * E].rearrange("p (i e) -> p i e", i=4)

        qT_w = sb("qT", [P, max(2 * K * X, RING * GT * P // 2)], F32)
        qT = qT_w[:, 0:RING * GT * P // 2].bitcast(F16).rearrange("p (l t n) -> p l t n", l=RING, t=GT)
        y0 = sb("y0", [P, GT, E], F32)
        y_w = sb("y_pair", [P, GT * E], F32)
        y_hi = y_w[:, 0:GT * E // 2].bitcast(F16).rearrange("p (i e) -> p i e", i=GT)
        y_lo = y_w[:, GT * E // 2:].bitcast(F16).rearrange("p (i e) -> p i e", i=GT)
        qkv = sb("qkv", [P, GT, 3, 2, D], F16)
        w_hi = sb("w_hi", [P, CH, NC], F16)
        w_lo = sb("w_lo", [P, CH, NC], F16)
        woT = sb("woT", [P, E + X], F32)
        en = sb("en", [P, 2, 2, D], F32)
        g_hi = sb("g_hi", [P, E + X], F16)
        g_lo = sb("g_lo", [P, E + X], F16)
        ident = sb("ident", [P, P], F32)
        ident16 = sb("ident16", [P, P], F16)
        zero16 = sb("zero16", [P, P], F16)
        stats = sb("stats", [P, GT, 6], F32)
        mv = sb("mv", [P, GT, 2], F32)
        stats1 = sb("stats1", [P, GT, 6], F32)
        mv1 = sb("mv1", [P, GT, 2], F32)
        vpe = sb("vpe", [P, GT], F32)
        rstd = sb("rstd", [P, GT], F32)
        rs = sb("rs", [P, GT], F32)
        nm = sb("nm", [P, GT], F32)
        nmr = sb("nmr", [P, GT], F32)
        mhalf = sb("mhalf", [P, K], F32)
        var0 = sb("var0", [P, K + GT], F32)
        var1 = sb("var1", [P, K], F32)
        lg = sb("lg", [P, K + TB, 2 * X], F32)

        bank = [pb(f"bank{i}", [P, 512], F32) for i in range(8)]
        p_xT, p_qkv, p_out, p_en, p_qT = bank[0:2], bank[2:4], bank[4:6], bank[6], bank[7]
        p_qT16 = p_qT[:, 0:P // 2].bitcast(F16)

        wall = big[0:D, 0:3 * E].rearrange("p (m e) -> p m e", m=3)
        wod = big[:, 3 * E:4 * E].rearrange("p (c r d) -> p c r d", c=CH, r=2)
        gw = big[:, 4 * E:4 * E + CH * X].rearrange("p (c j) -> p c j", c=CH)
        gwc = big[:, 5 * E:5 * E + CH * X].rearrange("p (c j) -> p c j", c=CH)
        inv_e = sb("inv_e", [P, P], F32)

        BX, KX = B * X, K * X
        gates = sb("gates", [P, KX], F32)
        work_a = sb("work_a", [P, KX], F32)
        work_b, work_c = qT_w[:, 0:KX], qT_w[:, KX:2 * KX]
        work_d, work_e = y0[:, :, :].rearrange("p i e -> p (i e)")[:, 0:KX], y_w[:, 0:KX]
        phalf = sb("phalf", [P, K], F32)
        sd0 = sb("sd0", [P, K], F32)
        r1 = sb("r1", [P, K], F32)
        row = sb("row", [P, K], F32)
        row_r = sb("row_r", [P, K], F32)
        pos_i = sb("pos_i", [P, K], I32)
        lo_i = sb("lo_i", [P, K], I32)
        hi_i = sb("hi_i", [P, K], I32)
        lo_f = sb("lo_f", [P, K], F32)
        hi_f = sb("hi_f", [P, K], F32)
        tok_a = sb("tok_a", [P, K], F32)
        tok_b = sb("tok_b", [P, K], F32)
        part = sb("part", [P, BX], F32)
        inv = sb("inv", [P, BX], F32)
        thr = sb("thr", [P, BX], I32)
        cand = sb("cand", [P, BX], I32)
        more = sb("more", [P, BX], I32)
        bit_f = sb("bit_f", [P, 1], F32)
        bit_i = sb("bit_i", [P, 1], I32)
        need = sb("need", [P, BX], F32)
        lim = sb("lim", [P, BX], F32)
        ev = sb("ev", [P, X], F32)
        one1 = sb("one1", [P, 1], F32)
        ones1 = sb("ones1", [P, P], F32)
        before = sb("before", [P, P], F32)
        tot = sb("tot", [P, X], F32)
        nt_f = sb("nt_f", [P, X], F32)
        nt_i = sb("nt_i", [P, X], I32)
        cum = sb("cum", [P, X], F32)
        start = sb("start", [P, X], F32)
        corr = sb("corr", [P, X], F32)
        nq_f = sb("nq_f", [P, 1], F32)
        nq_i = sb("nq_i", [P, 1], I32)
        iota_l = sb("iota_l", [P, P], F16)
        iota_t = sb("iota_t", [P, TABLE], F16)
        et_f = sb("et_f", [P, 2, TABLE], F32)
        et_i = sb("et_i", [P, TABLE], I32)
        tb_f = sb("tb_f", [P, TABLE], F32)
        tr_f = sb("tr_f", [P, TABLE], F32)
        tx_f = sb("tx_f", [P, TABLE], F32)
        table = sb("table", [P, TABLE], I32)
        oh_l = sb("oh_l", [P, GT, P], F16)
        oh_a = sb("oh_a", [P, GT, TABLE], F16)
        oh_b = sb("oh_b", [P, GT, TABLE], F16)
        idx_g = sb("idx_g", [P, GT], I32)
        idx_s = sb("idx_s", [P, GT], I32)

        x_v = x.rearrange("b (p g t) e -> b g p t e", p=P, t=GT)
        o_v = out.rearrange("b (p g t) e -> b g p t e", p=P, t=GT)

        s_w = sem("weights_loaded")
        s_const = sem("constants_made")
        s_setup_pe = sem("setup_products_done")
        s_setup_a = sem("setup_high_parts_done")
        s_setup_v = sem("setup_rests_done")
        s_ld = [sem(f"x_loaded{i}") for i in range(2)]
        s_st = [sem(f"x1_stored{i}") for i in range(2)]
        s_bn = sem("x_stats_done")
        s_mv = sem("x_moments_done")
        s_pool = sem("pool_chain")
        s_rs = sem("x_rstd_done")
        s_y = sem("y_done")
        s_T = sem("y_transposed")
        s_hi = sem("y_high_part_done")
        s_lo = sem("y_rest_done")
        s_qkv = sem("qkv_done")
        s_qh = sem("qkv_high_part_done")
        s_ql = sem("qkv_rest_done")
        s_qt = sem("energy_and_qT_done")
        s_qc = sem("qT_copied")
        s_en = sem("energy_summed")
        s_ec = sem("energy_copied")
        s_g = sem("g_product_done")
        s_gh = sem("g_high_part_done")
        s_gl = sem("g_rest_done")
        s_o = sem("attention_out_done")
        s_x1 = sem("x1_done")
        s_bn1 = sem("x1_stats_done")
        s_mv1 = sem("x1_moments_done")
        s_t = sem("moments_kept")

        s_ex = sem("experts_loaded")
        s_eh = sem("experts_high_part_done")
        s_el = sem("experts_rest_done")
        s_dve = sem("vector_chain")
        s_const2 = sem("constants2_made")
        s_sd = sem("deviations_done")
        s_part = sem("parts_of_sum_done")
        s_sum = sem("sum_done")
        s_oh = sem("one_hots_done")
        s_list = sem("one_hots_summed")
        s_table = sem("table_done")
        s_zero = sem("gather_places_zeroed")
        s_ga = [sem(f"gathered{i}") for i in range(4)]
        s_sc = [sem(f"scattered{i}") for i in range(4)]
        s_fbn = sem("row_stats_done")
        s_fmv = sem("row_moments_done")
        s_fpool = sem("pool_chain2")
        s_frs = sem("row_rstd_done")
        s_fy = sem("row_y_done")
        s_fT = sem("row_y_transposed")
        s_fhi = sem("row_high_part_done")
        s_flo = sem("row_rest_done")
        s_fmm = sem("row_product_done")
        s_fin = sem("row_sum_done")
        s_idx = sem("indices_copied")

        class Chain:

            def __init__(self, eng, sem):
                self.eng, self.sem, self.n = eng, sem, 0

            def __call__(self, ins, rounds=0):
                self.n += 1
                ins.then_inc(self.sem, 1)
                self.eng.wait_ge(self.sem, rounds + self.n)
                self.eng.nop(nofuse=True)

        def by_tile(a):
            return a.rearrange("p (b t j) -> p b t j", b=B, j=X)

        def to_tiles(a):
            return a.rearrange("p (b j) -> p b j", b=B).unsqueeze(2).to_broadcast([P, B, TB, X])

        ROUNDS, BITS = ITERS, 30

        block = ctx.enter_context(nc.Block())

        def steps(eng, body, start=None):
            with eng.Fori(0, GB) as g:
                body(g, True, False)
            with eng.Fori(1, B) as step:
                if start:
                    start(step)
                with eng.Fori(0, GB) as g:
                    body(step * GB + g, True, True)
            if start:
                start(B)
            with eng.Fori(0, GB) as g:
                body(g + B * GB, False, True)

        @block.sync
        def _(sp):
            for m, w in enumerate((wq, wk, wv)):
                sp.dma_start(wall[:, m], w).then_inc(s_w, 16)
            for r in range(2):
                sp.dma_start(wod[:, :, r], wo.rearrange("(c p) d -> p c d", p=P)).then_inc(s_w, 16)
            sp.dma_start(gw, gate_w[0].rearrange("(c p) j -> p c j", p=P)).then_inc(s_w, 16)
            sp.wait_ge(s_setup_pe, 5)
            sp.wait_ge(s_setup_v, 3)

            def load(L, i):
                sp.dma_start(xr[:, L % RING], x_v[L // GB, L % GB]).then_inc(s_ld[i], 16)

            def store(L, i):
                sp.wait_ge(s_x1, L * GT + GT + 2)
                sp.dma_start(o_v[L // GB, L % GB], xr[:, L % RING]).then_inc(s_st[i], 16)

            for i in range(2):
                sp.sem_inc(s_st[i], 16)
            load(0, 0)
            load(1, 1)
            with sp.Fori(1, GB // 2 + 1) as j:
                for i in range(2):
                    sp.wait_ge(s_T, (j * 2 + i - 1) * GT)
                    load(j * 2 + i, i)
            with sp.Fori(GB // 2 + 1, NG // 2) as j:
                for i in range(2):
                    sp.wait_ge(s_T, (j * 2 + i - 1) * GT)
                    sp.wait_ge(s_st[i], (j - GB // 2) * 16)
                    load(j * 2 + i, i)
                    store(j * 2 + i - GB - 2, i)
            sp.wait_ge(s_T, (NG - 1) * GT)
            sp.sem_inc(s_ld[0], 16)
            with sp.Fori(NG // 2 - GB // 2 - 1, NG // 2) as j:
                for i in range(2):
                    sp.wait_ge(s_st[i], (j + 1) * 16)
                    store(j * 2 + i, i)
            for i in range(2):
                sp.wait_ge(s_st[i], (NG // 2 + 1) * 16)
            sp.wait_ge(s_t, 2 * NG + 1)
            ex_v = experts.rearrange("x (c p) n -> p x c n", p=P)
            sp.dma_start(e_f, ex_v[:, 0:X // 2]).then_inc(s_ex, 16)
            sp.wait_ge(s_el, X)
            sp.dma_start(e_f, ex_v[:, X // 2:X]).then_inc(s_ex, 16)

        @block.gpsimd
        def _(pool):
            count = [0]

            def link(ins):
                count[0] += 1
                ins.then_inc(s_pool, 1)
                pool.wait_ge(s_pool, count[0])

            nc.gpsimd.memset(mhalf[:, :], -0.5)
            nc.gpsimd.memset(zero16[:, :], 0.0)
            nc.gpsimd.memset(inv_e[:, :], 1.0 / E)
            nc.gpsimd.memset(ident16[:, :], 0.0)
            link(nc.gpsimd.memset(ident[:, :], 0.0))
            for m in (ident, ident16):
                pool.affine_select(out=m[:, :], in_=m[:, :], compare_op=ALU.not_equal, fill=1.0, base=0,
                                   pattern=[[-1, P]], channel_multiplier=1).then_inc(s_const, 1)

            def rstd_of_group(L, first):
                pool.wait_ge(s_mv, (L + 1) * GT)
                pool.nop(nofuse=True)
                if not first:
                    pool.wait_ge(s_y, L * GT)
                    pool.nop(nofuse=True)
                base = count[0] if first else None
                ops = [
                    lambda: nc.gpsimd.tensor_scalar(vpe[:, :], mv[:, :, 1], LN_EPS, None, ALU.add),
                    lambda: nc.gpsimd.tensor_tensor(rstd[:, :], vpe[:, :], mhalf[:, 0:GT], ALU.pow),
                    lambda: nc.gpsimd.tensor_scalar(rs[:, :], rstd[:, :], SY, None, ALU.mult),
                    lambda: nc.gpsimd.tensor_scalar(nm[:, :], mv[:, :, 0], -1.0, None, ALU.mult),
                ]
                for n, op in enumerate(ops):
                    op().then_inc(s_pool, 1)
                    pool.wait_ge(s_pool, L * 4 + (count[0] + n + 1))
                    pool.nop(nofuse=True)
                nc.gpsimd.tensor_tensor(nmr[:, :], nm[:, :], rs[:, :], ALU.mult).then_inc(s_rs, 1)

            nc.gpsimd.memset(phalf[:, :], 0.5)
            nc.gpsimd.memset(one1[:, :], 1.0)
            nc.gpsimd.memset(ones1[:, :], 1.0)
            nc.gpsimd.iota(ev[:, :], [[1, X]], base=1, channel_multiplier=0, allow_small_or_imprecise_dtypes=True)
            nc.gpsimd.iota(iota_l[:, :], [[1, P]], base=0, channel_multiplier=0, allow_small_or_imprecise_dtypes=True)
            nc.gpsimd.iota(iota_t[:, :], [[1, TABLE]], base=0, channel_multiplier=0,
                           allow_small_or_imprecise_dtypes=True)
            nc.gpsimd.iota(tok_a[:, :], [[P, B], [0, TB]], base=0, channel_multiplier=1,
                           allow_small_or_imprecise_dtypes=True)
            nc.gpsimd.iota(tok_b[:, :], [[0, B], [1, TB]], base=1, channel_multiplier=0,
                           allow_small_or_imprecise_dtypes=True)
            nc.gpsimd.memset(before[:, :], 1.0).then_inc(s_const2, 1)
            pool.wait_ge(s_const2, 1)
            pool.affine_select(out=before[:, :], in_=before[:, :], compare_op=ALU.is_gt, fill=0.0, base=0,
                               pattern=[[1, P]], channel_multiplier=-1).then_inc(s_const2, 1)

            rstd_of_group(0, True)
            with pool.Fori(1, NG) as L:
                rstd_of_group(L, False)

            chain = Chain(pool, s_sd)
            pool.wait_ge(s_t, 2 * NG + 1)
            chain(nc.gpsimd.tensor_scalar(sd0[:, :], var0[:, 0:K], LN_EPS, None, ALU.add))
            chain(nc.gpsimd.tensor_scalar(r1[:, :], var1[:, :], LN_EPS, None, ALU.add))
            chain(nc.gpsimd.tensor_tensor(sd0[:, :], sd0[:, :], phalf[:, :], ALU.pow))
            chain(nc.gpsimd.tensor_tensor(r1[:, :], r1[:, :], mhalf[:, :], ALU.pow))

            for j in range(X):
                pool.wait_ge(s_eh, j + 1)
                f = e_f[:, j % (X // 2)]
                nc.gpsimd.tensor_scalar(f, f, SX, None, ALU.mult).then_inc(s_el, 1)
                pool.wait_ge(s_el, 2 * j + 1)
                nc.gpsimd.tensor_tensor(e_lo[:, j], f, e_hi[:, j], ALU.subtract).then_inc(s_el, 1)
            pool.wait_ge(s_el, 2 * X)
            nc.gpsimd.memset(big[:, half:half + 8 * E], 0.0).then_inc(s_zero, 1)
            nc.gpsimd.memset(idx_s[:, :], int(EMPTY)).then_inc(s_zero, 1)
            pool.wait_ge(s_zero, 2)

            rows = out.rearrange("b n e -> (b n) e")
            for i in range(2):
                pool.wait_ge(s_st[i], (NG // 2 + 1) * 16)
            pool.wait_ge(s_table, 3)
            nq = pool.value_load(nq_i[0:1, 0:1], min_val=1, max_val=TILES // 4)

            def gather(i, n):
                nc.gpsimd.tensor_copy(idx_g[:, i:i + 1], table[:, bass.ts(n, 1)]).then_inc(s_idx, 1)

            def gather_rows(i):
                pool.indirect_dma_start(xg[:, i], None, rows,
                                        bass.IndirectOffsetOnAxis(ap=idx_g[:, i:i + 1], axis=0),
                                        bounds_check=B * N - 1, oob_is_err=False).then_inc(s_ga[i], 16)

            def row_rstd(i, n):
                pool.wait_ge(s_fmv, n + 1)
                pool.nop(nofuse=True)
                ops = (
                    lambda: nc.gpsimd.tensor_scalar(vpe[:, i:i + 1], mv[:, i, 1:2], LN_EPS, None, ALU.add),
                    lambda: nc.gpsimd.tensor_tensor(rstd[:, i:i + 1], vpe[:, i:i + 1], mhalf[:, 0:1], ALU.pow),
                    lambda: nc.gpsimd.tensor_scalar(rs[:, i:i + 1], rstd[:, i:i + 1], SY, None, ALU.mult),
                    lambda: nc.gpsimd.tensor_scalar(nm[:, i:i + 1], mv[:, i, 0:1], -1.0, None, ALU.mult),
                )
                for q, op in enumerate(ops):
                    op().then_inc(s_fpool, 1)
                    pool.wait_ge(s_fpool, n * 4 + q + 1)
                    pool.nop(nofuse=True)
                nc.gpsimd.tensor_tensor(nmr[:, i:i + 1], nm[:, i:i + 1], rs[:, i:i + 1], ALU.mult).then_inc(s_frs, 1)

            def scatter(i):
                pool.indirect_dma_start(rows, bass.IndirectOffsetOnAxis(ap=idx_s[:, i:i + 1], axis=0), yo[:, i], None,
                                        bounds_check=B * N - 1, oob_is_err=False).then_inc(s_sc[i], 16)

            for i in range(4):
                scatter(i)
            for i in range(4):
                gather(i, i)
            pool.wait_ge(s_idx, 4)
            for i in range(4):
                gather_rows(i)
            row_rstd(0, 0)
            row_rstd(1, 1)
            with pool.Fori(0, TILES // 4) as q:
                with pool.If(q < nq):
                    for i in range(4):
                        n = q * 4 + i
                        row_rstd((i + 2) % 4, n + 2)
                        pool.wait_ge(s_ga[i], (q + 1) * 16)
                        pool.wait_ge(s_sc[i], (q + 1) * 16)
                        pool.nop(nofuse=True)
                        gather(i, n + 4)
                        nc.gpsimd.tensor_copy(idx_s[:, i:i + 1], table[:, bass.ts(n, 1)]).then_inc(s_idx, 1)
                        pool.wait_ge(s_idx, n * 2 + 6)
                        pool.wait_ge(s_fin, n + 3)
                        pool.nop(nofuse=True)
                        gather_rows(i)
                        scatter(i)
                with pool.Else():
                    pool.nop()
                pool.nop()
            for i in range(4):
                pool.wait_ge(s_sc[i], nq * 16 + 16)
                pool.nop(nofuse=True)
                pool.wait_ge(s_ga[i], nq * 16 + 16)
                pool.nop(nofuse=True)

        @block.scalar
        def _(act):
            for h in range(2):
                act.wait_ge(s_setup_pe, h + 1)
                for c in range(2):
                    ins = nc.scalar.activation(w_hi[:, 2 * h + c, 0:3 * D], bank[h][:, c * 3 * D:(c + 1) * 3 * D],
                                               ACT.Copy, scale=SW)
                ins.then_inc(s_setup_a, 1)
            nc.scalar.activation(w_hi[:, :, 3 * D:NC], gw, ACT.Copy, scale=SGATE).then_inc(s_setup_a, 1)
            act.wait_ge(s_setup_pe, 3)
            nc.scalar.activation(woT[:, 0:E], bank[2][:, :], ACT.Copy).then_inc(s_setup_a, 1)
            act.wait_ge(s_setup_pe, 5)
            nc.scalar.activation(woT[:, E:E + X], bank[4][:, 0:X], ACT.Copy).then_inc(s_setup_a, 1)

            def energy(step):
                act.wait_ge(s_en, step)
                for r in range(2):
                    nc.scalar.activation(en[:, :, r, :], p_en[:, 0:P].rearrange("p (a d) -> p a d", a=2),
                                         ACT.Copy).then_inc(s_ec, 1)
                act.wait_ge(s_g, step)
                nc.scalar.activation(g_hi[:, 0:E], p_out[0][:, :], ACT.Copy, scale=OUT_SCALE / (SQ * SQ))
                nc.scalar.activation(g_hi[:, E:E + X], p_out[1][:, 0:X], ACT.Copy,
                                     scale=OUT_SCALE * SLOG / (SQ * SQ)).then_inc(s_gh, 1)

            def body(L, a1, a2):
                k = L * GT
                if not a1:
                    return

                def high(i):
                    act.wait_ge(s_T, k + i + 1)
                    nc.scalar.activation(y_hi[:, i], p_xT[i % 2][:, :], ACT.Copy).then_inc(s_hi, 1)

                def qkv_high(i):
                    act.wait_ge(s_qkv, k + i + 1)
                    nc.scalar.activation(qkv[:, i, :, 0, :], p_qkv[i % 2][:, 0:3 * D].rearrange("p (m d) -> p m d", m=3),
                                         ACT.Copy, scale=SQ / (SY * SW)).then_inc(s_qh, 1)

                def copy_qT(i):
                    act.wait_ge(s_qt, k + i + 1)
                    act.nop(nofuse=True)
                    nc.scalar.activation(qT[:, L % RING, i], p_qT16, ACT.Copy).then_inc(s_qc, 1)

                act.wait_ge(s_rs, L + 1)
                act.nop(nofuse=True)
                for i in range(GT):
                    nc.scalar.activation(y0[:, i], xr[:, L % RING, i], ACT.Identity, bias=nmr[:, i:i + 1],
                                         scale=rs[:, i:i + 1]).then_inc(s_y, 1)
                high(0)
                high(1)
                high(2)
                qkv_high(0)
                high(3)
                qkv_high(1)
                copy_qT(0)
                qkv_high(2)
                copy_qT(1)
                qkv_high(3)
                copy_qT(2)
                copy_qT(3)

            with act.Fori(0, GB) as g:
                body(g, True, False)
            with act.Fori(1, B) as step:
                energy(step)
                with act.Fori(0, GB) as g:
                    body(step * GB + g, True, True)
            energy(B)

            for j in range(X):
                act.wait_ge(s_ex, 16 if j < X // 2 else 32)
                nc.scalar.activation(e_hi[:, j], e_f[:, j % (X // 2)], ACT.Copy, scale=SX).then_inc(s_eh, 1)

            act.wait_ge(s_table, 3)
            nq = act.value_load(nq_i[0:1, 0:1], min_val=1, max_val=TILES // 4)

            def row_y(i, n):
                act.wait_ge(s_frs, n + 1)
                nc.scalar.activation(y0[:, i], xg[:, i], ACT.Identity, bias=nmr[:, i:i + 1],
                                     scale=rs[:, i:i + 1]).then_inc(s_fy, 1)

            def row_high(i, n):
                act.wait_ge(s_fT, n + 1)
                nc.scalar.activation(y_hi[:, i], p_xT[i % 2][:, :], ACT.Copy).then_inc(s_fhi, 1)

            row_y(0, 0)
            row_high(0, 0)
            with act.Fori(0, TILES // 4) as q:
                with act.If(q < nq):
                    for i in range(4):
                        row_y((i + 1) % 4, q * 4 + i + 1)
                        row_high((i + 1) % 4, q * 4 + i + 1)
                with act.Else():
                    act.nop()
                act.nop()

        @block.vector
        def _(dve):
            for h in range(2):
                dve.wait_ge(s_setup_a, h + 1)
                for c in range(2):
                    ins = nc.vector.scalar_tensor_tensor(
                        w_lo[:, 2 * h + c, 0:3 * D], bank[h][:, c * 3 * D:(c + 1) * 3 * D], SW,
                        w_hi[:, 2 * h + c, 0:3 * D], ALU.mult, ALU.subtract)
                ins.then_inc(s_setup_v, 1)
            dve.wait_ge(s_setup_a, 3)
            nc.vector.scalar_tensor_tensor(w_lo[:, :, 3 * D:NC], gw, SGATE, w_hi[:, :, 3 * D:NC],
                                           ALU.mult, ALU.subtract)
            dve.wait_ge(s_setup_pe, 4)
            nc.vector.tensor_tensor(gwc, gw, bank[3][:, 0:X].unsqueeze(1).to_broadcast([P, CH, X]),
                                    ALU.subtract).then_inc(s_setup_v, 1)

            def moments(L, first=False):
                pass

            def x_stats(L, i):
                if i == 0:
                    pass
                nc.vector.bn_stats(stats[:, i], xr[:, L % RING, i]).then_inc(s_bn, 1)

            def x_moments(L):
                for i in range(GT):
                    dve.wait_ge(s_bn, L * GT + i + 1)
                    dve.nop(nofuse=True)
                    nc.vector.bn_aggr(mv[:, i], stats[:, i]).then_inc(s_mv, 1)
                dve.wait_ge(s_mv, L * GT + GT)
                dve.nop(nofuse=True)
                nc.vector.tensor_copy(var0[:, bass.ts(L, GT)], mv[:, :, 1]).then_inc(s_t, 1)

            def energy(step):
                dve.wait_ge(s_gh, step)
                nc.vector.scalar_tensor_tensor(g_lo[:, 0:E], p_out[0][:, :], OUT_SCALE / (SQ * SQ), g_hi[:, 0:E],
                                               ALU.mult, ALU.subtract)
                nc.vector.scalar_tensor_tensor(g_lo[:, E:E + X], p_out[1][:, 0:X], OUT_SCALE * SLOG / (SQ * SQ),
                                               g_hi[:, E:E + X], ALU.mult, ALU.subtract).then_inc(s_gl, 1)

            def body(L, a1, a2, ahead=None):
                k = L * GT
                M = L - GB
                m = M * GT

                def rest(i):
                    if a1:
                        dve.wait_ge(s_hi, k + i + 1)
                        nc.vector.tensor_tensor(y_lo[:, i], p_xT[i % 2][:, :], y_hi[:, i],
                                                ALU.subtract).then_inc(s_lo, 1)

                def qkv_rest(i):
                    if a1:
                        dve.wait_ge(s_qh, k + i + 1)
                        nc.vector.scalar_tensor_tensor(
                            qkv[:, i, :, 1, :], p_qkv[i % 2][:, 0:3 * D].rearrange("p (m d) -> p m d", m=3),
                            SQ / (SY * SW), qkv[:, i, :, 0, :], ALU.mult, ALU.subtract)
                        w = slice(0, 2 * X if a2 else X)
                    else:
                        dve.wait_ge(s_qkv, k + i + 1)
                        dve.nop(nofuse=True)
                        w = slice(X, 2 * X)
                    nc.vector.tensor_copy(lg[:, k + i, w], p_qkv[i % 2][:, 3 * D + w.start:3 * D + w.stop]).then_inc(s_ql, 1)

                def add(i):
                    if a2:
                        dve.wait_ge(s_o, m + i + 1)
                        nc.vector.scalar_tensor_tensor(xr[:, M % RING, i], p_out[i % 2][:, :], 1.0 / SQ,
                                                       xr[:, M % RING, i], ALU.mult, ALU.add).then_inc(s_x1, 1)

                def ahead_stats(i):
                    if a1:
                        nc.vector.bn_stats(stats[:, i], xr[:, (L + 1) % RING, i]).then_inc(s_bn, 1)

                add(0)
                rest(0)
                add(1)
                rest(1)
                if a1:
                    dve.wait_ge(*ahead)
                    dve.nop(nofuse=True)
                ahead_stats(0)
                ahead_stats(1)
                rest(2)
                qkv_rest(0)
                ahead_stats(2)
                rest(3)
                qkv_rest(1)
                ahead_stats(3)
                if a1:
                    x_moments(L + 1)
                add(2)
                qkv_rest(2)
                add(3)
                qkv_rest(3)
                if a2:
                    for i in range(GT):
                        dve.wait_ge(s_x1, m + i + 3)
                        dve.nop(nofuse=True)
                        nc.vector.bn_stats(stats1[:, i], xr[:, M % RING, i]).then_inc(s_bn1, 1)
                    for i in range(GT):
                        dve.wait_ge(s_bn1, m + i + 1)
                        dve.nop(nofuse=True)
                        nc.vector.bn_aggr(mv1[:, i], stats1[:, i]).then_inc(s_mv1, 1)
                    dve.wait_ge(s_mv1, m + GT)
                    dve.nop(nofuse=True)
                    nc.vector.tensor_copy(var1[:, bass.ts(M, GT)], mv1[:, :, 1]).then_inc(s_t, 1)

            def pair(L, a2):
                body(L, True, a2, (s_ld[1], (L // 2 + 1) * 16))
                body(L + 1, True, a2, (s_ld[0], (L // 2 + 2) * 16))

            dve.wait_ge(s_ld[0], 16)
            for i in range(GT):
                nc.vector.bn_stats(stats[:, i], xr[:, 0, i]).then_inc(s_bn, 1)
            x_moments(0)
            with dve.Fori(0, GB // 2) as g:
                pair(g * 2, False)
            with dve.Fori(1, B) as step:
                energy(step)
                with dve.Fori(0, GB // 2) as g:
                    pair(step * GB + g * 2, True)
            energy(B)
            with dve.Fori(0, GB) as g:
                body(g + B * GB, False, True)

            chain = Chain(dve, s_dve)
            V = nc.vector
            A, Bw, Cw, Dw, Ew = work_a[:, :], work_b, work_c, work_d, work_e
            G = gates[:, :]

            def tiles(a):
                return a.rearrange("p (k j) -> p k j", j=X)

            def rows_(a):
                return a.unsqueeze(2).to_broadcast([P, K, X])

            def sums(a):
                return V.tensor_reduce(part[:, :].rearrange("p (b j) -> p b j", b=B),
                                       a.rearrange("p (b t j) -> p b j t", b=B, j=X), AX.X, ALU.add)

            total = bank[0][:, 0:BX]

            dve.wait_ge(s_sd, 4)
            dve.wait_ge(s_t, 2 * NG + 1)
            dve.wait_ge(s_const2, 2)
            chain(V.tensor_tensor(tiles(A), lg[:, 0:K, 0:X], rows_(sd0[:, :]), ALU.mult))
            chain(V.scalar_tensor_tensor(tiles(A), lg[:, TB:TB + K, X:2 * X], SY * SGATE / (SQ * SLOG), tiles(A),
                                         ALU.mult, ALU.add))
            chain(V.tensor_tensor(tiles(A), tiles(A), rows_(r1[:, :]), ALU.mult))
            chain(V.tensor_scalar(G, A, 1.0 / (SY * SGATE), CLIP_EPS, ALU.mult, ALU.max))

            with dve.Fori(0, ROUNDS) as r:
                n0 = chain.n
                sums(G).then_inc(s_part, 1)
                dve.wait_ge(s_sum, r + 1)
                chain(V.reciprocal(inv[:, :], total), r * 5)
                chain(V.tensor_tensor(by_tile(G), by_tile(G), to_tiles(inv[:, :]), ALU.mult), r * 5)
                chain(V.tensor_reduce(row[:, :], tiles(G), AX.X, ALU.add), r * 5)
                chain(V.reciprocal(row_r[:, :], row[:, :]), r * 5)
                chain(V.tensor_tensor(tiles(G), tiles(G), rows_(row_r[:, :]), ALU.mult), r * 5)
                assert chain.n - n0 == 5
            chain.n += (ROUNDS - 1) * 5

            V.memset(thr[:, :], 0)
            chain(V.memset(bit_f[:, :], float(1 << (BITS - 1))))
            chain(V.tensor_copy(bit_i[:, :], bit_f[:, :]))
            with dve.Fori(0, BITS) as r:
                n0 = chain.n
                chain(V.tensor_tensor(cand[:, :], thr[:, :], bit_i[:, :].to_broadcast([P, BX]), ALU.bitwise_or), r * 6)
                chain(V.tensor_tensor(by_tile(A), by_tile(G), to_tiles(cand[:, :].bitcast(F32)), ALU.is_ge), r * 6)
                sums(A).then_inc(s_part, 1)
                dve.wait_ge(s_sum, ROUNDS + r + 1)
                chain(V.tensor_scalar(more[:, :], total, CAP - 0.5, bit_f[:, :], ALU.is_ge, ALU.mult), r * 6)
                chain(V.tensor_tensor(thr[:, :], thr[:, :], more[:, :], ALU.bitwise_or), r * 6)
                chain(V.tensor_scalar(bit_f[:, :], bit_f[:, :], 0.5, None, ALU.mult), r * 6)
                chain(V.tensor_copy(bit_i[:, :], bit_f[:, :]), r * 6)
                assert chain.n - n0 == 6
            chain.n += (BITS - 1) * 6

            def by_row(a):
                return a.rearrange("p (b j t) -> p b t j", b=B, j=X)

            def in_rows(a):
                return a.rearrange("p (r t) -> p r t", t=TB)

            threshold = to_tiles(thr[:, :].bitcast(F32))
            above, equal, prefix = A, Bw, Cw
            chain(V.tensor_tensor(by_tile(above), by_tile(G), threshold, ALU.is_gt))
            sums(above).then_inc(s_part, 1)
            dve.wait_ge(s_sum, ROUNDS + BITS + 1)
            chain(V.tensor_scalar(need[:, :], total, -1.0, float(CAP), ALU.mult, ALU.add))
            chain(V.tensor_tensor(by_row(equal), by_tile(G), threshold, ALU.is_equal))
            chain(V.tensor_tensor_scan(prefix, one1[:, :].to_broadcast([P, KX]), equal, 0.0, ALU.mult, ALU.add))
            chain(V.tensor_reduce(part[:, :], in_rows(equal), AX.X, ALU.add))
            chain(V.tensor_tensor(lim[:, :], in_rows(prefix)[:, :, TB - 1], part[:, :], ALU.subtract))
            chain(V.scalar_tensor_tensor(lim[:, :], lim[:, :], 1.0, need[:, :], ALU.add, ALU.add))
            V.engine_nop().then_inc(s_part, 1)
            dve.wait_ge(s_sum, ROUNDS + BITS + 2)
            chain(V.tensor_tensor(lim[:, :], lim[:, :], total, ALU.subtract))
            chain(V.tensor_tensor(in_rows(prefix), in_rows(prefix), lim[:, :].unsqueeze(2).to_broadcast([P, BX, TB]),
                                  ALU.is_lt))
            chain(V.tensor_tensor(equal, equal, prefix, ALU.mult))
            chosen = A
            chain(V.tensor_tensor(by_tile(chosen), by_tile(above), by_row(equal), ALU.add))

            score, active = Bw, Cw
            chain(V.tensor_tensor(tiles(score), tiles(chosen), ev[:, :].unsqueeze(1).to_broadcast([P, K, X]), ALU.mult))
            chain(V.tensor_reduce(row[:, :], tiles(score), AX.X, ALU.max))
            chain(V.tensor_tensor(tiles(score), tiles(score), rows_(row[:, :]), ALU.is_equal))
            chain(V.scalar_tensor_tensor(chosen, G, 0.5, chosen, ALU.is_gt, ALU.mult))

            def by_expert(a):
                return a.rearrange("p (j k) -> p k j", j=X)

            chain(V.tensor_tensor(by_expert(active), tiles(score), tiles(chosen), ALU.mult))

            prefix = Dw
            chain(V.tensor_tensor_scan(prefix, one1[:, :].to_broadcast([P, KX]), active, 0.0, ALU.mult, ALU.add))
            chain(V.tensor_reduce(part[:, 0:X], active.rearrange("p (j k) -> p j k", j=X), AX.X, ALU.add))
            V.engine_nop().then_inc(s_part, 1)
            dve.wait_ge(s_sum, ROUNDS + BITS + 3)
            chain(V.tensor_scalar(nt_i[:, :], bank[0][:, X:2 * X], P - 1.0, None, ALU.add))
            chain(V.tensor_single_scalar(nt_i[:, :], nt_i[:, :], 7, ALU.arith_shift_right))
            chain(V.tensor_copy(nt_f[:, :], nt_i[:, :]))
            chain(V.tensor_tensor_scan(cum[:, :], one1[:, :].to_broadcast([P, X]), nt_f[:, :], 0.0, ALU.mult, ALU.add))
            chain(V.tensor_tensor(start[:, :], cum[:, :], nt_f[:, :], ALU.subtract))
            chain(V.tensor_scalar(nq_i[:, :], cum[:, X - 1:X], 1.0, 3.0, ALU.max, ALU.add))
            V.tensor_single_scalar(nq_i[:, :], nq_i[:, :], 2, ALU.arith_shift_right).then_inc(s_table, 1)
            ends = prefix.rearrange("p (j k) -> p j k", j=X)[:, :, K - 1]
            chain(V.tensor_tensor(corr[:, :], part[:, 0:X], ends, ALU.subtract))
            chain(V.scalar_tensor_tensor(corr[:, :], start[:, :], float(P), corr[:, :], ALU.mult, ALU.add))
            chain(V.tensor_tensor(corr[:, :], corr[:, :], bank[0][:, 0:X], ALU.add))

            def experts_(a):
                return a.rearrange("p (j k) -> p j k", j=X)

            chain(V.tensor_tensor(experts_(prefix), experts_(prefix), corr[:, :].unsqueeze(2).to_broadcast([P, X, K]),
                                  ALU.add))
            chain(V.tensor_tensor(prefix, prefix, active, ALU.mult))
            chain(V.tensor_reduce(row[:, :], by_expert(prefix), AX.X, ALU.add))
            chain(V.tensor_scalar(pos_i[:, :], row[:, :], -1.0, None, ALU.add))
            V.tensor_single_scalar(lo_i[:, :], pos_i[:, :], P - 1, ALU.bitwise_and)
            chain(V.tensor_single_scalar(hi_i[:, :], pos_i[:, :], 7, ALU.arith_shift_right))
            V.tensor_copy(lo_f[:, :], lo_i[:, :])
            chain(V.tensor_copy(hi_f[:, :], hi_i[:, :]))

            chain(V.memset(et_f[:, 0], 0.0))
            for j in range(1, X):
                chain(V.scalar_tensor_tensor(et_f[:, j % 2], iota_t[:, :], start[:, j:j + 1], et_f[:, (j + 1) % 2],
                                             ALU.is_ge, ALU.add))
            V.tensor_copy(et_i[:, :], et_f[:, (X - 1) % 2]).then_inc(s_table, 1)

            with dve.Fori(0, K // GT) as r:
                dve.wait_ge(s_list, r + 1)
                for i in range(GT):
                    k1 = bass.ts(r * GT + i, 1)
                    V.tensor_scalar(oh_l[:, i], iota_l[:, :], lo_f[:, k1], None, ALU.is_equal)
                    V.tensor_scalar(oh_a[:, i], iota_t[:, :], hi_f[:, k1], tok_a[:, k1], ALU.is_equal, ALU.mult)
                    ins = V.tensor_scalar(oh_b[:, i], iota_t[:, :], hi_f[:, k1], tok_b[:, k1], ALU.is_equal, ALU.mult)
                ins.then_inc(s_oh, 1)
            dve.wait_ge(s_list, K // GT + 1)
            chain(V.tensor_copy(tb_f[:, :], bank[2][:, 0:TABLE]))
            chain(V.scalar_tensor_tensor(tr_f[:, :], bank[1][:, 0:TABLE], float(TB), tb_f[:, :], ALU.mult, ALU.add))
            chain(V.tensor_scalar(tx_f[:, :], tb_f[:, :], 0.0, EMPTY + 1.0, ALU.is_equal, ALU.mult))
            V.scalar_tensor_tensor(table[:, :], tr_f[:, :], -1.0, tx_f[:, :], ALU.add, ALU.add).then_inc(s_table, 1)

            dve.wait_ge(s_table, 3)
            nq = dve.value_load(nq_i[0:1, 0:1], min_val=1, max_val=TILES // 4)

            def row_stats(i, n, q):
                dve.wait_ge(s_ga[i], q * 16 + 16)
                dve.nop(nofuse=True)
                V.bn_stats(stats[:, i], xg[:, i]).then_inc(s_fbn, 1)
                dve.wait_ge(s_fbn, n + 1)
                dve.nop(nofuse=True)
                V.bn_aggr(mv[:, i], stats[:, i]).then_inc(s_fmv, 1)

            def row_rest(i, n):
                dve.wait_ge(s_fhi, n + 1)
                V.tensor_tensor(y_lo[:, i], p_xT[i % 2][:, :], y_hi[:, i], ALU.subtract).then_inc(s_flo, 1)

            row_stats(0, 0, 0)
            row_stats(1, 1, 0)
            row_rest(0, 0)
            with dve.Fori(0, TILES // 4) as q:
                with dve.If(q < nq):
                    for i in range(4):
                        n = q * 4 + i
                        row_stats((i + 2) % 4, n + 2, q + (i + 2) // 4)
                        row_rest((i + 1) % 4, n + 1)
                        dve.wait_ge(s_sc[i], q * 16 + 16)
                        dve.wait_ge(s_fmm, n + 1)
                        V.scalar_tensor_tensor(yo[:, i], p_out[i % 2][:, :], 1.0 / (SY * SX), xg[:, i],
                                               ALU.mult, ALU.add).then_inc(s_fin, 1)
                with dve.Else():
                    dve.nop()
                dve.nop()

        @block.tensor
        def _(pe):
            pe.sem_inc(s_lo, 2)
            pe.sem_inc(s_ql, 2)
            pe.sem_inc(s_qc, 1)
            pe.sem_inc(s_x1, 2)
            pe.sem_inc(s_fin, 2)
            pe.wait_ge(s_const, 2)
            pe.wait_ge(s_w, 16 * 6)
            for h in range(2):
                for c in range(2):
                    for m in range(3):
                        ins = nc.tensor.transpose(bank[h][:, c * 3 * D + m * D:c * 3 * D + (m + 1) * D],
                                                  wall[:, m, (2 * h + c) * P:(2 * h + c + 1) * P], ident[0:D, 0:D])
                ins.then_inc(s_setup_pe, 1)
            for c in range(CH):
                ins = nc.tensor.transpose(bank[2][:, c * P:(c + 1) * P], wod[:, c].rearrange("p r d -> p (r d)"),
                                          ident[:, :])
            ins.then_inc(s_setup_pe, 1)
            for c in range(CH):
                ins = nc.tensor.matmul(bank[3][:, 0:X], inv_e[:, :], gw[:, c], start=c == 0, stop=c == CH - 1)
            ins.then_inc(s_setup_pe, 1)
            pe.wait_ge(s_setup_v, 3)
            for c in range(CH):
                ins = nc.tensor.matmul(bank[4][:, 0:X], wod[:, c].rearrange("p r d -> p (r d)"), gwc[:, c],
                                       start=c == 0, stop=c == CH - 1)
            ins.then_inc(s_setup_pe, 1)
            pe.wait_ge(s_setup_a, 5)

            def zero_energy(start):
                return nc.tensor.matmul(p_en[:, 0:P], zero16[:, :], zero16[:, :], start=start, stop=not start)

            def energy(step):
                pe.wait_ge(s_ec, step * 2)
                pe.wait_ge(s_x1, (step - 1) * TB + 2)
                for a in range(2):
                    nc.tensor.matmul(p_out[0][:, :], en[:, a].rearrange("p r d -> p (r d)"), woT[:, 0:E],
                                     start=a == 0, stop=a == 1)
                for a in range(2):
                    ins = nc.tensor.matmul(p_out[1][:, 0:X], en[:, a].rearrange("p r d -> p (r d)"), woT[:, E:E + X],
                                           start=a == 0, stop=a == 1)
                ins.then_inc(s_g, 1)
                pe.wait_ge(s_gl, step)

            def body(L, a1, a2):
                k = L * GT
                M = L - GB
                m = M * GT

                def transpose(i):
                    if a1:
                        pe.wait_ge(s_lo, k + i + 1)
                        pe.wait_ge(s_y, k + i + 1)
                        for c in range(CH):
                            ins = nc.tensor.transpose(p_xT[i % 2][:, c * P:(c + 1) * P], y0[:, i, c * P:(c + 1) * P],
                                                      ident[:, :])
                        ins.then_inc(s_T, 1)

                def attend(i):
                    if a2:
                        pe.wait_ge(s_x1, m + i + 1)
                        pe.nop(nofuse=True)
                        for g, first in ((g_hi, True), (g_lo, False)):
                            ins = nc.tensor.matmul(p_out[i % 2][:, :], qT[:, M % RING, i], g[:, 0:E],
                                                   start=first, stop=not first)
                        ins.then_inc(s_o, 1)

                def project(i):
                    pe.wait_ge(s_ql, k + i + 1)
                    pe.nop(nofuse=True)
                    if a1:
                        pe.wait_ge(s_lo, k + i + 3)
                        for c in range(CH):
                            f = slice(c * P, (c + 1) * P)
                            nc.tensor.matmul(p_qkv[i % 2][:, 0:NC], y_hi[:, i, f], w_hi[:, c], start=c == 0, stop=False)
                            nc.tensor.matmul(p_qkv[i % 2][:, 0:NC], y_hi[:, i, f], w_lo[:, c], start=False, stop=False)
                            ins = nc.tensor.matmul(p_qkv[i % 2][:, 0:NC], y_lo[:, i, f], w_hi[:, c], start=False,
                                                   stop=c == CH - 1)
                    if a2:
                        for g, first in ((g_hi, True), (g_lo, False)):
                            ins = nc.tensor.matmul(p_qkv[i % 2][:, NC:NC + X], qT[:, M % RING, i], g[:, E:E + X],
                                                   start=first, stop=not first)
                    ins.then_inc(s_qkv, 1)

                def energy_and_qT(i):
                    if a1:
                        pe.wait_ge(s_ql, k + i + 3)
                        pe.wait_ge(s_qc, k + i + 1)
                        nc.tensor.transpose(p_qT16, qkv[:, i, 0].rearrange("p a d -> p (a d)"), ident16[:, :])
                        nc.tensor.matmul(p_en[:, 0:P], qkv[:, i, 2].rearrange("p a d -> p (a d)"),
                                         qkv[:, i, 1].rearrange("p a d -> p (a d)"), start=False,
                                         stop=False).then_inc(s_qt, 1)

                transpose(0)
                transpose(1)
                attend(0)
                attend(1)
                transpose(2)
                project(0)
                transpose(3)
                project(1)
                energy_and_qT(0)
                attend(2)
                project(2)
                energy_and_qT(1)
                attend(3)
                project(3)
                energy_and_qT(2)
                energy_and_qT(3)

            zero_energy(True)
            with pe.Fori(0, GB) as g:
                body(g, True, False)
            zero_energy(False).then_inc(s_en, 1)
            with pe.Fori(1, B) as step:
                energy(step)
                zero_energy(True)
                with pe.Fori(0, GB) as g:
                    body(step * GB + g, True, True)
                zero_energy(False).then_inc(s_en, 1)
            energy(B)
            with pe.Fori(0, GB) as g:
                body(g + B * GB, False, True)

            with pe.Fori(0, ROUNDS + BITS + 1) as r:
                pe.wait_ge(s_part, r + 1)
                nc.tensor.matmul(bank[0][:, 0:BX], ones1[:, :], part[:, :], start=True, stop=True).then_inc(s_sum, 1)
            pe.wait_ge(s_part, ROUNDS + BITS + 2)
            nc.tensor.matmul(bank[0][:, 0:BX], before[:, :], part[:, :], start=True, stop=True).then_inc(s_sum, 1)
            pe.wait_ge(s_part, ROUNDS + BITS + 3)
            nc.tensor.matmul(bank[0][:, 0:X], before[:, :], part[:, 0:X], start=True, stop=True)
            nc.tensor.matmul(bank[0][:, X:2 * X], ones1[:, :], part[:, 0:X], start=True, stop=True).then_inc(s_sum, 1)

            def zero_list(start):
                for n in (1, 2):
                    for a in range(0, TABLE, P):
                        w = min(P, TABLE - a)
                        ins = nc.tensor.matmul(bank[n][:, a:a + w], zero16[:, :], zero16[:, 0:w],
                                               start=start and a == 0, stop=not start and a + w == TABLE,
                                               skip_group_check=True)
                return ins

            zero_list(True).then_inc(s_list, 1)
            with pe.Fori(0, K // GT) as r:
                pe.wait_ge(s_oh, r + 1)
                for i in range(GT):
                    for n, oh in ((1, oh_a), (2, oh_b)):
                        ins = nc.tensor.matmul(bank[n][:, 0:TABLE], oh_l[:, i], oh[:, i], start=False, stop=False,
                                               skip_group_check=True)
                ins.then_inc(s_list, 1)

            pe.wait_ge(s_table, 3)
            pe.wait_ge(s_el, 2 * X)
            nq = pe.value_load(nq_i[0:1, 0:1], min_val=1, max_val=TILES // 4)

            def row_transpose(i, n):
                pe.wait_ge(s_fy, n + 1)
                for c in range(CH):
                    ins = nc.tensor.transpose(p_xT[i % 2][:, c * P:(c + 1) * P], y0[:, i, c * P:(c + 1) * P], ident[:, :])
                ins.then_inc(s_fT, 1)

            row_transpose(0, 0)
            with pe.Fori(0, TILES // 4) as q:
                with pe.If(q < nq):
                    for i in range(4):
                        n = q * 4 + i
                        j = pe.value_load(et_i[0:1, bass.ts(n, 1)], min_val=0, max_val=X - 1)
                        row_transpose((i + 1) % 4, n + 1)
                        pe.wait_ge(s_flo, n + 1)
                        pe.wait_ge(s_fin, n + 1)
                        for c in range(CH):
                            f = slice(c * P, (c + 1) * P)
                            nc.tensor.matmul(p_out[i % 2][:, :], y_hi[:, i, f], e_hi[:, j, c], start=c == 0, stop=False)
                            nc.tensor.matmul(p_out[i % 2][:, :], y_hi[:, i, f], e_lo[:, j, c], start=False, stop=False)
                            ins = nc.tensor.matmul(p_out[i % 2][:, :], y_lo[:, i, f], e_hi[:, j, c], start=False,
                                                   stop=c == CH - 1)
                        ins.then_inc(s_fmm, 1)
                with pe.Else():
                    pe.nop()
                pe.nop()


_INS = ["L0_attn_x", "L0_attn_wq", "L0_attn_wk", "L0_attn_wv", "L0_attn_wo", "L0_ffn_gate_w", "L0_ffn_experts"]


def kernel(**inputs):
    import numpy as _np
    import concourse.bacc as _bacc
    from concourse import mybir as _mybir
    from concourse.bass_utils import run_bass_kernel_spmd as _run

    nc = _bacc.Bacc("TRN2", target_bir_lowering=False, num_devices=1)
    arrays, args = {}, []
    for name in _INS:
        a = _np.ascontiguousarray(inputs[name])
        arrays[f"in_{name}_dram"] = a
        args.append(nc.dram_tensor(f"in_{name}_dram", a.shape, _mybir.dt.from_np(a.dtype), kind="ExternalInput").ap())
    shape = inputs["L0_attn_x"].shape
    args.append(nc.dram_tensor("out_0_dram", shape, _mybir.dt.float32, kind="ExternalOutput").ap())
    linear_attention_moe_kernel(nc, *args)
    r = _run(nc, [arrays], core_ids=[0])
    return r.results[0]["out_0_dram"]
```

```python
from contextlib import ExitStack


def linear_attention_moe_kernel(nc, x, wq, wk, wv, wo, gate_w, experts, out):
    import concourse.bass as bass
    from concourse import mybir

    F32, F16, I32 = mybir.dt.float32, mybir.dt.float16, mybir.dt.int32
    ALU, ACT, AX = mybir.AluOpType, mybir.ActivationFunctionType, mybir.AxisListType

    P = 128
    B, N, E = x.shape
    D = wq.shape[0]
    X = experts.shape[0]
    CH = E // P
    TB = N // P
    K = B * TB
    GT = 4
    GB = TB // GT
    NG = B * GB
    RING = GB + 4
    CAP = N // X
    LN_EPS, CLIP_EPS, ITERS = 1e-5, 1e-6, 8
    OUT_SCALE = (3.0 / D) ** 0.5

    SY, SW, SQ, SGATE, SLOG, SX = 64.0, 256.0, 64.0, 16.0, 1.0 / 16, 16.0
    NC = 3 * D + X
    TILES = -(-(K + X) // 4) * 4
    AHEAD = 8
    TABLE = TILES + AHEAD
    WIN = CAP // P + 1
    WX = WIN * X
    HT = TB // 2
    EMPTY = float(1 << 20)

    ctx = ExitStack()
    with ctx:
        def sb(name, shape, dt):
            return ctx.enter_context(nc.sbuf_tensor(name, shape, dt))

        def pb(name, shape, dt):
            return ctx.enter_context(nc.psum_tensor(name, shape, dt))

        def sem(name):
            return ctx.enter_context(nc.semaphore(name))

        ROUNDS, BITS, BB = ITERS, 30, 5
        big = sb("big", [P, RING * GT * E], F32)
        xr = big[:, :].rearrange("p (l t e) -> p l t e", l=RING, t=GT)
        HE = X * CH * E // 2
        e_hi = big[:, 0:HE].bitcast(F16).rearrange("p (x c n) -> p x c n", x=X, c=CH)
        e_lo = big[:, HE:2 * HE].bitcast(F16).rearrange("p (x c n) -> p x c n", x=X, c=CH)
        half = 2 * HE
        e_f = big[:, half:half + HE].rearrange("p (x c n) -> p x c n", x=X // 2, c=CH)
        xg = big[:, half:half + AHEAD * E].rearrange("p (i e) -> p i e", i=AHEAD)
        yo = big[:, half + AHEAD * E:half + (AHEAD + 4) * E].rearrange("p (i e) -> p i e", i=4)

        qT_w = sb("qT", [P, max(2 * K * X, RING * GT * P // 2)], F32)
        qT = qT_w[:, 0:RING * GT * P // 2].bitcast(F16).rearrange("p (l t n) -> p l t n", l=RING, t=GT)
        y0 = sb("y0", [P, GT, E], F32)
        y_w = sb("y_pair", [P, GT * E], F32)
        y_hi = y_w[:, 0:GT * E // 2].bitcast(F16).rearrange("p (i e) -> p i e", i=GT)
        y_lo = y_w[:, GT * E // 2:].bitcast(F16).rearrange("p (i e) -> p i e", i=GT)
        qkv = sb("qkv", [P, GT, 3, 2, D], F16)
        w_hi = sb("w_hi", [P, CH, NC], F16)
        w_lo = sb("w_lo", [P, CH, NC], F16)
        woT = sb("woT", [P, E + X], F32)
        en = sb("en", [P, 2, 2, D], F32)
        g_hi = sb("g_hi", [P, E + X], F16)
        g_lo = sb("g_lo", [P, E + X], F16)
        ident = sb("ident", [P, P], F32)
        ident16 = sb("ident16", [P, P], F16)
        zero16 = sb("zero16", [P, P], F16)
        stats = sb("stats", [P, 2, GT, 6], F32)
        mv = sb("mv", [P, 2, GT, 2], F32)
        sum1 = sb("sum1", [P, GT], F32)
        nmean1 = sb("nmean1", [P, GT], F32)
        ssq1 = sb("ssq1", [P, GT], F32)
        vpe1 = sb("vpe1", [P, GT], F32)
        squares = sb("squares", [P, GT, E], F16)
        vpe = sb("vpe", [P, GT], F32)
        rstd = sb("rstd", [P, GT], F32)
        rs = sb("rs", [P, 2, GT], F32)
        nm = sb("nm", [P, GT], F32)
        nmr = sb("nmr", [P, 2, GT], F32)
        mhalf = sb("mhalf", [P, GT], F32)
        LG = max(K + TB, (2 * P + 6 * WX) * HT // (4 * X) + 1)
        lg = sb("lg", [P, LG, 2 * X], F32)

        bank = [pb(f"bank{i}", [P, 512], F32) for i in range(8)]
        p_xT, p_qkv, p_out, p_en, p_qT = bank[0:2], bank[2:4], bank[4:6], bank[6], bank[7]
        p_qT16 = p_qT[:, 0:P // 2].bitcast(F16)

        wall = big[0:D, 0:3 * E].rearrange("p (m e) -> p m e", m=3)
        wod = big[:, 3 * E:4 * E].rearrange("p (c r d) -> p c r d", c=CH, r=2)
        gw = big[:, 4 * E:4 * E + CH * X].rearrange("p (c j) -> p c j", c=CH)
        gwc = big[:, 5 * E:5 * E + CH * X].rearrange("p (c j) -> p c j", c=CH)
        inv_e = sb("inv_e", [P, P], F32)

        BX, KX = B * X, K * X
        gates = sb("gates", [P, KX], F32)
        work_a = sb("work_a", [P, KX], F32)
        work_b, work_c = qT_w[:, 0:KX], qT_w[:, KX:2 * KX]
        work_d = y0[:, :, :].rearrange("p i e -> p (i e)")[:, 0:KX]
        g_halves = gates[:, :].rearrange("p (b h t j) -> p h t b j", b=B, h=2, t=HT)
        g_order = work_a[:, :].rearrange("p (t h b j) -> p t h b j", t=HT, h=2, b=B)
        gT = y_w[0:2 * BX, 0:HT * P]
        sd0 = sb("sd0", [P, K + 2 * GT], F32)
        r1 = sb("r1", [P, K], F32)
        row = sb("row", [P, K], F32)
        row_r = sb("row_r", [P, K], F32)
        m_max = sb("m_max", [P, K], F16)
        pos_i = sb("pos_i", [P, K], I32)
        lo_i = sb("lo_i", [P, K], I32)
        hi_i = sb("hi_i", [P, K], I32)
        lo16 = sb("lo16", [P, K], F16)
        hi16 = sb("hi16", [P, K], F16)
        tok_a = sb("tok_a", [P, B], F32)
        tok_b = sb("tok_b", [P, TB], F16)
        part = sb("part", [P, BX], F32)
        inv = sb("inv", [P, BX], F32)
        pair = sb("pair", [P, P], F16)
        bits_f = sb("bits_f", [P, BITS + 1], F32)
        bits_i = sb("bits_i", [P, BITS + 1], I32)
        cand = sb("cand", [P, 1], I32)
        cand_x = sb("cand_x", [P, 1], I32)
        fail = sb("fail", [P, 1], I32)
        cnt = sb("cnt", [P, 1], F16)
        need1 = sb("need1", [P, 1], F32)
        spread = sb("spread", [P, 2, P], F32)
        thr_need = sb("thr_need", [P, 2, BX], F32)
        prev = sb("prev", [P, BX], F32)
        excl = sb("excl", [P, BX], F32)
        base_i = sb("base_i", [P, BX], I32)
        tile_i = sb("tile_i", [P, BX], I32)
        off_i = sb("off_i", [P, BX], I32)
        tile_f = sb("tile_f", [P, BX], F32)
        off_f = sb("off_f", [P, BX], F32)
        need = sb("need", [P, BX], F32)
        lim = sb("lim", [P, BX], F32)
        win_x = sb("win_x", [P, X], F32)
        one1 = sb("one1", [P, 1], F32)
        ones1 = sb("ones1", [P, P], F32)
        before = sb("before", [P, P], F32)
        tot = sb("tot", [P, X], F32)
        nt_f = sb("nt_f", [P, X], F32)
        nt_i = sb("nt_i", [P, X], I32)
        cum = sb("cum", [P, X], F32)
        start = sb("start", [P, X], F32)
        corr = sb("corr", [P, X], F32)
        nq_f = sb("nq_f", [P, 1], F32)
        nq_i = sb("nq_i", [P, 1], I32)
        iota_t = sb("iota_t", [P, TABLE], F16)
        iota_l = squares[:, :, :].rearrange("p i e -> p (i e)")[:, 0:P * HT].rearrange("p (l t) -> p l t", l=P)
        iota_c = sb("iota_c", [P, WX, HT], F16)
        mask_a = sb("mask_a", [P, X], F32)
        mask_b = sb("mask_b", [P, X], F32)
        mask = sb("mask", [P, X], F32)
        win_f = sb("win_f", [P, X], F32)
        win_s = sb("win_s", [P, 1], F32)
        scale_s = sb("scale_s", [P, 1], F32)
        sel = sb("sel", [P, X * B], F32)
        dest = sb("dest", [P, B], F32)
        et_f = sb("et_f", [P, 2, TABLE], F32)
        et_i = sb("et_i", [P, TABLE], I32)
        empty = sb("empty", [P, TABLE], F32)
        table = sb("table", [P, TABLE], I32)
        lg16 = lg[:, :, :].rearrange("p k j -> p (k j)").bitcast(F16)
        oh_l = lg16[:, 0:2 * P * HT].rearrange("p (h l t) -> p h l t", h=2, l=P)
        oh_w = lg16[:, 2 * P * HT:2 * P * HT + 4 * WX * HT].rearrange("p (h q c t) -> p h q c t", h=2, q=2, c=WX)
        eq_w = lg16[:, 2 * P * HT + 4 * WX * HT:2 * P * HT + 6 * WX * HT].rearrange("p (h c t) -> p h c t", h=2, c=WX)
        win_list = sb("win_list", [P, B, P], F16)
        oh_t = work_c[:, 0:B * TABLE // 2].bitcast(F16).rearrange("p (b n) -> p b n", b=B)
        idx_g = sb("idx_g", [P, AHEAD], I32)
        idx_s = sb("idx_s", [P, GT], I32)

        x_v = x.rearrange("b (p g t) e -> b g p t e", p=P, t=GT)
        o_v = out.rearrange("b (p g t) e -> b g p t e", p=P, t=GT)

        s_w = sem("weights_loaded")
        s_const = sem("constants_made")
        s_setup_pe = sem("setup_products_done")
        s_setup_a = sem("setup_high_parts_done")
        s_setup_v = sem("setup_rests_done")
        s_ld = [sem(f"x_loaded{i}") for i in range(2)]
        s_st = [sem(f"x1_stored{i}") for i in range(2)]
        s_bn = sem("x_stats_done")
        s_mv = sem("x_moments_done")
        s_pool = sem("pool_chain")
        s_rs = sem("x_rstd_done")
        s_y = sem("y_done")
        s_T = sem("y_transposed")
        s_hi = sem("y_high_part_done")
        s_lo = sem("y_rest_done")
        s_qkv = sem("qkv_done")
        s_qh = sem("qkv_high_part_done")
        s_ql = sem("qkv_rest_done")
        s_qt = sem("energy_and_qT_done")
        s_qc = sem("qT_copied")
        s_en = sem("energy_summed")
        s_ec = sem("energy_copied")
        s_g = sem("g_product_done")
        s_gh = sem("g_high_part_done")
        s_gl = sem("g_rest_done")
        s_o = sem("attention_out_done")
        s_x1 = sem("x1_done")
        s_nm1 = sem("x1_means_done")
        s_sq = sem("x1_squares_summed")
        s_pool1 = sem("pool_chain1")
        s_r1 = sem("x1_rstd_done")

        s_ex = sem("experts_loaded")
        s_eh = sem("experts_high_part_done")
        s_el = sem("experts_rest_done")
        s_dve = sem("vector_chain")
        s_const2 = sem("constants2_made")
        s_sd = sem("deviations_done")
        s_part = sem("parts_of_sum_done")
        s_sum = sem("sum_done")
        s_gates = sem("gates_done")
        s_go = sem("gates_ordered")
        s_gt = sem("gates_transposed")
        s_gc = sem("gates_copied")
        s_cnt = sem("count_parts_done")
        s_tot = sem("count_done")
        s_eq = sem("window_one_hots_done")
        s_ea = sem("window_one_hots_scaled")
        s_oh = sem("one_hots_done")
        s_list = sem("one_hots_summed")
        s_wl = sem("window_list_copied")
        s_dest = sem("places_of_windows_done")
        s_tab = sem("table_summed")
        s_table = sem("table_done")
        s_zero = sem("gather_places_zeroed")
        s_ga = [sem(f"gathered{i}") for i in range(AHEAD)]
        s_sc = [sem(f"scattered{i}") for i in range(4)]
        s_fbn = sem("row_stats_done")
        s_fmv = sem("row_moments_done")
        s_fvar = sem("row_variance_done")
        s_frs = sem("row_rstd_done")
        s_fy = sem("row_y_done")
        s_fT = sem("row_y_transposed")
        s_fhi = sem("row_high_part_done")
        s_flo = sem("row_rest_done")
        s_fmm = sem("row_product_done")
        s_fin = sem("row_sum_done")
        s_idx = sem("indices_copied")

        class Chain:

            def __init__(self, eng, sem):
                self.eng, self.sem, self.n = eng, sem, 0

            def __call__(self, ins, rounds=0):
                self.n += 1
                ins.then_inc(self.sem, 1)
                self.eng.wait_ge(self.sem, rounds + self.n)
                self.eng.nop(nofuse=True)

        def by_tile(a):
            return a.rearrange("p (b t j) -> p b t j", b=B, j=X)

        def to_tiles(a):
            return a.rearrange("p (b j) -> p b j", b=B).unsqueeze(2).to_broadcast([P, B, TB, X])

        block = ctx.enter_context(nc.Block())

        def steps(eng, body, start=None):
            with eng.Fori(0, GB) as g:
                body(g, True, False)
            with eng.Fori(1, B) as step:
                if start:
                    start(step)
                with eng.Fori(0, GB) as g:
                    body(step * GB + g, True, True)
            if start:
                start(B)
            with eng.Fori(0, GB) as g:
                body(g + B * GB, False, True)

        @block.sync
        def _(sp):
            for m, w in enumerate((wq, wk, wv)):
                sp.dma_start(wall[:, m], w).then_inc(s_w, 16)
            for r in range(2):
                sp.dma_start(wod[:, :, r], wo.rearrange("(c p) d -> p c d", p=P)).then_inc(s_w, 16)
            sp.dma_start(gw, gate_w[0].rearrange("(c p) j -> p c j", p=P)).then_inc(s_w, 16)
            sp.wait_ge(s_setup_pe, 5)
            sp.wait_ge(s_setup_v, 3)

            def load(L, i):
                sp.dma_start(xr[:, L % RING], x_v[L // GB, L % GB]).then_inc(s_ld[i], 16)

            def store(L, i):
                sp.wait_ge(s_x1, L * GT + GT + 2)
                sp.nop(nofuse=True)
                sp.dma_start(o_v[L // GB, L % GB], xr[:, L % RING]).then_inc(s_st[i], 16)
                sp.wait_ge(s_sq, L * GT + GT * 2)
                sp.nop(nofuse=True)

            load(0, 0)
            load(1, 1)
            with sp.Fori(1, RING // 2) as j:
                for i in range(2):
                    sp.wait_ge(s_bn, (j * 2 + i - 1) * GT)
                    sp.nop(nofuse=True)
                    load(j * 2 + i, i)
            with sp.Fori(RING // 2, NG // 2) as j:
                for i in range(2):
                    store((j - RING // 2) * 2 + i, i)
                    sp.wait_ge(s_st[i], (j - RING // 2 + 1) * 16)
                    sp.nop(nofuse=True)
                    sp.wait_ge(s_bn, (j * 2 + i - 1) * GT)
                    sp.nop(nofuse=True)
                    load(j * 2 + i, i)
            for i in range(2):
                sp.wait_ge(s_bn, (NG - 1 + i) * GT)
                sp.nop(nofuse=True)
                sp.sem_inc(s_ld[i], 16)
            with sp.Fori((NG - RING) // 2, NG // 2) as j:
                for i in range(2):
                    store(j * 2 + i, i)
                    sp.wait_ge(s_st[i], (j + 1) * 16)
                    sp.nop(nofuse=True)
            sp.wait_ge(s_mv, (NG + 2) * GT)
            sp.wait_ge(s_y, K + 3)
            ex_v = experts.rearrange("x (c p) n -> p x c n", p=P)
            sp.dma_start(e_f, ex_v[:, 0:X // 2]).then_inc(s_ex, 16)
            sp.wait_ge(s_el, X)
            sp.dma_start(e_f, ex_v[:, X // 2:X]).then_inc(s_ex, 16)

        @block.gpsimd
        def _(pool):
            count = [0]

            def link(ins):
                count[0] += 1
                ins.then_inc(s_pool, 1)
                pool.wait_ge(s_pool, count[0])

            nc.gpsimd.memset(mhalf[:, :], -0.5)
            nc.gpsimd.memset(zero16[:, :], 0.0)
            nc.gpsimd.memset(inv_e[:, :], 1.0 / E)
            nc.gpsimd.memset(ident16[:, :], 0.0)
            link(nc.gpsimd.memset(ident[:, :], 0.0))
            for m in (ident, ident16):
                pool.affine_select(out=m[:, :], in_=m[:, :], compare_op=ALU.not_equal, fill=1.0, base=0,
                                   pattern=[[-1, P]], channel_multiplier=1).then_inc(s_const, 1)

            def rstd_of_group(L, h, first=False):
                pool.wait_ge(s_mv, (L + 1) * GT)
                pool.nop(nofuse=True)
                if not first:
                    pool.wait_ge(s_y, (L - 1) * GT)
                    pool.wait_ge(s_sd, L)
                    pool.nop(nofuse=True)
                ops = [
                    lambda: nc.gpsimd.tensor_scalar(vpe[:, :], mv[:, h, :, 1], LN_EPS, None, ALU.add),
                    lambda: nc.gpsimd.tensor_tensor(rstd[:, :], vpe[:, :], mhalf[:, :], ALU.pow),
                    lambda: nc.gpsimd.tensor_scalar(rs[:, h], rstd[:, :], SY, None, ALU.mult),
                    lambda: nc.gpsimd.tensor_scalar(nm[:, :], mv[:, h, :, 0], -1.0, None, ALU.mult),
                ]
                for n, op in enumerate(ops):
                    op().then_inc(s_pool, 1)
                    pool.wait_ge(s_pool, L * 4 + (count[0] + n + 1))
                    pool.nop(nofuse=True)
                nc.gpsimd.tensor_tensor(nmr[:, h], nm[:, :], rs[:, h], ALU.mult).then_inc(s_rs, 1)
                nc.gpsimd.tensor_tensor(sd0[:, bass.ts(L, GT)], vpe[:, :], rstd[:, :], ALU.mult).then_inc(s_sd, 1)

            def rstd1_of_group(M):
                pool.wait_ge(s_sq, (M + 2) * GT)
                pool.wait_ge(s_r1, M + 1)
                pool.nop(nofuse=True)
                nc.gpsimd.tensor_scalar(vpe1[:, :], ssq1[:, :], 1.0 / E, LN_EPS, ALU.mult, ALU.add).then_inc(s_pool1, 1)
                pool.wait_ge(s_pool1, M + 1)
                pool.nop(nofuse=True)
                nc.gpsimd.tensor_tensor(r1[:, bass.ts(M, GT)], vpe1[:, :], mhalf[:, :], ALU.pow).then_inc(s_r1, 1)

            nc.gpsimd.memset(one1[:, :], 1.0)
            nc.gpsimd.memset(ones1[:, :], 1.0)
            I = dict(allow_small_or_imprecise_dtypes=True)
            nc.gpsimd.iota(win_x[:, :], [[P * WIN, X]], base=0, channel_multiplier=0, **I)
            nc.gpsimd.iota(iota_t[:, :], [[1, TABLE]], base=0, channel_multiplier=0, **I)
            nc.gpsimd.iota(iota_c[:, :, :], [[1, WX], [0, HT]], base=0, channel_multiplier=0, **I)
            nc.gpsimd.iota(tok_a[:, :], [[P, B]], base=0, channel_multiplier=1, **I)
            nc.gpsimd.iota(tok_b[:, :], [[1, TB]], base=1, channel_multiplier=0, **I)
            nc.gpsimd.iota(win_f[:, :], [[-WIN, X]], base=0, channel_multiplier=1, **I)
            for r in range(BITS):
                nc.gpsimd.memset(bits_f[:, r:r + 1], float(1 << (BITS - 1 - r)))
            nc.gpsimd.memset(bits_f[:, BITS:BITS + 1], 0.0)
            nc.gpsimd.memset(mask_a[:, :], 1.0)
            nc.gpsimd.memset(mask_b[:, :], 1.0)
            nc.gpsimd.memset(pair[:, :], 0.0)
            nc.gpsimd.memset(before[:, :], 1.0).then_inc(s_const2, 1)
            pool.wait_ge(s_const2, 1)
            pool.affine_select(out=before[:, :], in_=before[:, :], compare_op=ALU.is_gt, fill=0.0, base=0,
                               pattern=[[1, P]], channel_multiplier=-1)
            for q, m in enumerate((mask_a, mask_b)):
                pool.affine_select(out=m[:, :], in_=m[:, :], compare_op=ALU.is_ge, fill=0.0, base=-q * WX,
                                   pattern=[[-WIN, X]], channel_multiplier=1)
            nc.gpsimd.tensor_copy(bits_i[:, :], bits_f[:, :])
            pool.affine_select(out=pair[:, :], in_=pair[:, :], compare_op=ALU.not_equal, fill=1.0, base=0,
                               pattern=[[-1, P]], channel_multiplier=1).then_inc(s_const2, 1)
            pool.wait_ge(s_const2, 2)
            for q, m in enumerate((mask_a, mask_b)):
                pool.affine_select(out=m[:, :], in_=m[:, :], compare_op=ALU.is_ge, fill=0.0, base=q * WX + WIN - 1,
                                   pattern=[[WIN, X]], channel_multiplier=-1)
            pool.affine_select(out=pair[:, :], in_=pair[:, :], compare_op=ALU.not_equal, fill=1.0, base=BX,
                               pattern=[[-1, P]], channel_multiplier=1).then_inc(s_const2, 1)
            pool.wait_ge(s_const2, 3)
            pool.affine_select(out=pair[:, :], in_=pair[:, :], compare_op=ALU.not_equal, fill=1.0, base=-BX,
                               pattern=[[-1, P]], channel_multiplier=1).then_inc(s_const2, 1)

            pool.sem_inc(s_r1, 1)
            rstd_of_group(0, 0, True)
            pool.wait_ge(s_sd, 1)
            rstd_of_group(1, 1, True)
            with pool.Fori(1, GB // 2 + 1) as j:
                for h in range(2):
                    rstd_of_group(j * 2 + h, h)
            with pool.Fori(GB // 2 + 1, NG // 2 + 1) as j:
                for h in range(2):
                    rstd_of_group(j * 2 + h, h)
                    rstd1_of_group(j * 2 + h - GB - 2)
            with pool.Fori(NG - GB, NG) as M:
                rstd1_of_group(M)

            nc.gpsimd.iota(iota_l, [[1, P], [0, HT]], base=0, channel_multiplier=0, **I).then_inc(s_const2, 1)

            for j in range(X):
                pool.wait_ge(s_eh, j + 1)
                f = e_f[:, j % (X // 2)]
                nc.gpsimd.tensor_scalar(f, f, SX, None, ALU.mult).then_inc(s_el, 1)
                pool.wait_ge(s_el, 2 * j + 1)
                nc.gpsimd.tensor_tensor(e_lo[:, j], f, e_hi[:, j], ALU.subtract).then_inc(s_el, 1)
            pool.wait_ge(s_el, 2 * X)
            nc.gpsimd.memset(big[:, half:half + (AHEAD + 4) * E], 0.0).then_inc(s_zero, 1)
            nc.gpsimd.memset(idx_s[:, :], int(EMPTY)).then_inc(s_zero, 1)
            pool.wait_ge(s_zero, 2)

            rows = out.rearrange("b n e -> (b n) e")
            for i in range(2):
                pool.wait_ge(s_st[i], NG // 2 * 16)
            pool.wait_ge(s_table, 3)
            nq = pool.value_load(nq_i[0:1, 0:1], min_val=1, max_val=TILES // 4)

            def gather(j):
                pool.indirect_dma_start(xg[:, j], None, rows,
                                        bass.IndirectOffsetOnAxis(ap=idx_g[:, j:j + 1], axis=0),
                                        bounds_check=B * N - 1, oob_is_err=False).then_inc(s_ga[j], 16)

            def row_rstd(i, n):
                pool.wait_ge(s_fvar, n + 1)
                pool.nop(nofuse=True)
                nc.gpsimd.tensor_tensor(rstd[:, i:i + 1], vpe[:, i:i + 1], mhalf[:, 0:1], ALU.pow).then_inc(s_frs, 1)

            def scatter(i):
                pool.indirect_dma_start(rows, bass.IndirectOffsetOnAxis(ap=idx_s[:, i:i + 1], axis=0), yo[:, i], None,
                                        bounds_check=B * N - 1, oob_is_err=False).then_inc(s_sc[i], 16)

            for i in range(4):
                scatter(i)
            pool.wait_ge(s_idx, 1)
            for j in range(AHEAD):
                gather(j)
            for i in range(4):
                row_rstd(i, i)
            with pool.Fori(0, -(-TILES // AHEAD)) as r:
                for h in range(2):
                    with pool.If(r * 2 + h < nq):
                        for i in range(4):
                            n = r * AHEAD + h * 4 + i
                            row_rstd(i, n + 4)
                            pool.wait_ge(s_fin, n + 3)
                            pool.nop(nofuse=True)
                            pool.wait_ge(s_idx, n + 2)
                            pool.nop(nofuse=True)
                            scatter(i)
                            gather(h * 4 + i)
                    with pool.Else():
                        pool.nop()
                    pool.nop()
            for i in range(4):
                pool.wait_ge(s_sc[i], nq * 16 + 16)
                pool.nop(nofuse=True)
            for j in range(AHEAD):
                pool.wait_ge(s_ga[j], (nq + (1 - j // 4)) // 2 * 16 + 16)
                pool.nop(nofuse=True)

        @block.scalar
        def _(act):
            for h in range(2):
                act.wait_ge(s_setup_pe, h + 1)
                for c in range(2):
                    ins = nc.scalar.activation(w_hi[:, 2 * h + c, 0:3 * D], bank[h][:, c * 3 * D:(c + 1) * 3 * D],
                                               ACT.Copy, scale=SW)
                ins.then_inc(s_setup_a, 1)
            nc.scalar.activation(w_hi[:, :, 3 * D:NC], gw, ACT.Copy, scale=SGATE).then_inc(s_setup_a, 1)
            act.wait_ge(s_setup_pe, 3)
            nc.scalar.activation(woT[:, 0:E], bank[2][:, :], ACT.Copy).then_inc(s_setup_a, 1)
            act.wait_ge(s_setup_pe, 5)
            nc.scalar.activation(woT[:, E:E + X], bank[4][:, 0:X], ACT.Copy).then_inc(s_setup_a, 1)

            def energy(step):
                act.wait_ge(s_en, step)
                for r in range(2):
                    nc.scalar.activation(en[:, :, r, :], p_en[:, 0:P].rearrange("p (a d) -> p a d", a=2),
                                         ACT.Copy).then_inc(s_ec, 1)
                act.wait_ge(s_g, step)
                nc.scalar.activation(g_hi[:, 0:E], p_out[0][:, :], ACT.Copy, scale=OUT_SCALE / (SQ * SQ))
                nc.scalar.activation(g_hi[:, E:E + X], p_out[1][:, 0:X], ACT.Copy,
                                     scale=OUT_SCALE * SLOG / (SQ * SQ)).then_inc(s_gh, 1)

            def y(n, L, i, h):
                if i == 0:
                    act.wait_ge(s_rs, L + 1)
                    act.nop(nofuse=True)
                nc.scalar.activation(y0[:, i], xr[:, L % RING, i], ACT.Identity, bias=nmr[:, h, i:i + 1],
                                     scale=rs[:, h, i:i + 1]).then_inc(s_y, 1)

            def high(n, i):
                act.wait_ge(s_T, n + 1)
                nc.scalar.activation(y_hi[:, i], p_xT[i % 2][:, :], ACT.Copy).then_inc(s_hi, 1)

            def body(L, h, a1, a2):
                k = L * GT
                M = L - GB
                m = M * GT

                def square(i):
                    if a2:
                        if i == 0:
                            act.wait_ge(s_r1, M + 1)
                        act.wait_ge(s_nm1, m + i + 1)
                        act.nop(nofuse=True)
                        nc.scalar.activation(squares[:, i], xr[:, M % RING, i], ACT.Square, bias=nmean1[:, i:i + 1],
                                             accum_out=ssq1[:, i:i + 1]).then_inc(s_sq, 1)

                def qkv_high(i):
                    act.wait_ge(s_qkv, k + i + 1)
                    nc.scalar.activation(qkv[:, i, :, 0, :], p_qkv[i % 2][:, 0:3 * D].rearrange("p (m d) -> p m d", m=3),
                                         ACT.Copy, scale=SQ / (SY * SW)).then_inc(s_qh, 1)

                def copy_qT(i):
                    act.wait_ge(s_qt, k + i + 1)
                    act.nop(nofuse=True)
                    nc.scalar.activation(qT[:, L % RING, i], p_qT16, ACT.Copy).then_inc(s_qc, 1)

                for i in range(GT):
                    if a1:
                        if i > 0:
                            copy_qT(i - 1)
                        qkv_high(i)
                        high(k + i + 2, (i + 2) % GT)
                        y(k + i + 3, L + (i + 3) // GT, (i + 3) % GT, (h + (i + 3) // GT) % 2)
                    square(i)
                if a1:
                    copy_qT(GT - 1)

            act.sem_inc(s_sq, GT)
            for i in range(3):
                y(i, 0, i, 0)
            high(0, 0)
            high(1, 1)
            with act.Fori(0, GB // 2) as g:
                for h in range(2):
                    body(g * 2 + h, h, True, False)
            with act.Fori(1, B) as step:
                energy(step)
                with act.Fori(0, GB // 2) as g:
                    for h in range(2):
                        body(step * GB + g * 2 + h, h, True, True)
            energy(B)
            with act.Fori(0, GB) as g:
                body(g + B * GB, 0, False, True)

            for j in range(X):
                act.wait_ge(s_ex, 16 if j < X // 2 else 32)
                nc.scalar.activation(e_hi[:, j], e_f[:, j % (X // 2)], ACT.Copy, scale=SX).then_inc(s_eh, 1)

            act.wait_ge(s_gates, 1)
            for q in range(4):
                for h in range(2):
                    t = slice(q * HT // 4, (q + 1) * HT // 4)
                    ins = nc.scalar.activation(g_order[:, t, h], g_halves[:, h, t], ACT.Copy)
                ins.then_inc(s_go, 1)
            for q in range(4):
                act.wait_ge(s_gt, q + 1)
                w = HT * P // 4
                nc.scalar.activation(gT[:, q * w:(q + 1) * w], bank[1 + q][0:2 * BX, 0:w], ACT.Copy).then_inc(s_gc, 1)
            with act.Fori(0, B) as b:
                for h in range(2):
                    act.wait_ge(s_eq, b * 2 + h + 1)
                    act.wait_ge(s_list, b * 2 + h + 1)
                    act.nop(nofuse=True)
                    nc.scalar.activation(oh_w[:, h, 0], eq_w[:, h], ACT.Copy, scale=tok_a[:, bass.ds(b, 1)]).then_inc(s_ea, 1)
                act.wait_ge(s_list, b * 2 + 4)
                act.nop(nofuse=True)
                nc.scalar.activation(win_list[0:2 * WX, bass.ds(b, 1)], bank[1][0:2 * WX, 0:P], ACT.Copy).then_inc(s_wl, 1)

            act.wait_ge(s_table, 3)
            nq = act.value_load(nq_i[0:1, 0:1], min_val=1, max_val=TILES // 4)

            def row_high(i, n):
                act.wait_ge(s_fT, n + 1)
                nc.scalar.activation(y_hi[:, i], p_xT[i % 2][:, :], ACT.Copy).then_inc(s_fhi, 1)

            nc.scalar.activation(idx_g[:, :], table[:, 0:AHEAD], ACT.Copy).then_inc(s_idx, 1)
            row_high(0, 0)
            row_high(1, 1)
            with act.Fori(0, -(-TILES // AHEAD)) as r:
                for h in range(2):
                    with act.If(r * 2 + h < nq):
                        for i in range(4):
                            n = r * AHEAD + h * 4 + i
                            j = h * 4 + i
                            act.wait_ge(s_ga[j], r * 16 + 16)
                            act.wait_ge(s_sc[i], (r * 2 + h + 1) * 16)
                            act.nop(nofuse=True)
                            nc.scalar.activation(idx_g[:, j:j + 1], table[:, bass.ds(n + AHEAD, 1)], ACT.Copy)
                            nc.scalar.activation(idx_s[:, i:i + 1], table[:, bass.ds(n, 1)], ACT.Copy).then_inc(s_idx, 1)
                            row_high((i + 2) % 4, n + 2)
                    with act.Else():
                        act.nop()
                    act.nop()

        @block.vector
        def _(dve):
            for h in range(2):
                dve.wait_ge(s_setup_a, h + 1)
                for c in range(2):
                    ins = nc.vector.scalar_tensor_tensor(
                        w_lo[:, 2 * h + c, 0:3 * D], bank[h][:, c * 3 * D:(c + 1) * 3 * D], SW,
                        w_hi[:, 2 * h + c, 0:3 * D], ALU.mult, ALU.subtract)
                ins.then_inc(s_setup_v, 1)
            dve.wait_ge(s_setup_a, 3)
            nc.vector.scalar_tensor_tensor(w_lo[:, :, 3 * D:NC], gw, SGATE, w_hi[:, :, 3 * D:NC],
                                           ALU.mult, ALU.subtract)
            dve.wait_ge(s_setup_pe, 4)
            nc.vector.tensor_tensor(gwc, gw, bank[3][:, 0:X].unsqueeze(1).to_broadcast([P, CH, X]),
                                    ALU.subtract).then_inc(s_setup_v, 1)

            def x_stats(L, i, h):
                nc.vector.bn_stats(stats[:, h, i], xr[:, L % RING, i]).then_inc(s_bn, 1)

            def x_moments(L, h):
                for i in range(GT):
                    dve.wait_ge(s_bn, L * GT + i + 1)
                    dve.nop(nofuse=True)
                    nc.vector.bn_aggr(mv[:, h, i], stats[:, h, i]).then_inc(s_mv, 1)

            def rest(n, i):
                dve.wait_ge(s_hi, n + 1)
                nc.vector.tensor_tensor(y_lo[:, i], p_xT[i % 2][:, :], y_hi[:, i], ALU.subtract).then_inc(s_lo, 1)

            def energy(step):
                dve.wait_ge(s_gh, step)
                nc.vector.scalar_tensor_tensor(g_lo[:, 0:E], p_out[0][:, :], OUT_SCALE / (SQ * SQ), g_hi[:, 0:E],
                                               ALU.mult, ALU.subtract)
                nc.vector.scalar_tensor_tensor(g_lo[:, E:E + X], p_out[1][:, 0:X], OUT_SCALE * SLOG / (SQ * SQ),
                                               g_hi[:, E:E + X], ALU.mult, ALU.subtract).then_inc(s_gl, 1)

            def body(L, h, a1, a2):
                k = L * GT
                M = L - GB
                m = M * GT

                def qkv_rest(i):
                    if a1:
                        dve.wait_ge(s_qh, k + i + 1)
                        nc.vector.scalar_tensor_tensor(
                            qkv[:, i, :, 1, :], p_qkv[i % 2][:, 0:3 * D].rearrange("p (m d) -> p m d", m=3),
                            SQ / (SY * SW), qkv[:, i, :, 0, :], ALU.mult, ALU.subtract)
                        w = slice(0, 2 * X if a2 else X)
                    else:
                        dve.wait_ge(s_qkv, k + i + 1)
                        dve.nop(nofuse=True)
                        w = slice(X, 2 * X)
                    nc.vector.tensor_copy(lg[:, k + i, w], p_qkv[i % 2][:, 3 * D + w.start:3 * D + w.stop]).then_inc(s_ql, 1)

                def add(i):
                    if a2:
                        dve.wait_ge(s_sq, m + i + 1)
                        dve.nop(nofuse=True)
                        dve.wait_ge(s_o, m + i + 1)
                        nc.vector.scalar_tensor_tensor(xr[:, M % RING, i], p_out[i % 2][:, :], 1.0 / SQ,
                                                       xr[:, M % RING, i], ALU.mult, ALU.add,
                                                       accum_out=sum1[:, i:i + 1]).then_inc(s_x1, 1)

                def mean(i):
                    if a2:
                        dve.wait_ge(s_x1, m + i + 3)
                        nc.vector.tensor_scalar(nmean1[:, i:i + 1], sum1[:, i:i + 1], -1.0 / E, None,
                                                ALU.mult).then_inc(s_nm1, 1)

                for i in range(GT):
                    add(i)
                    if a1 and i == 0:
                        dve.wait_ge(s_ld[h], (L // 2 + 2) * 16)
                        dve.wait_ge(s_rs, L + 1)
                        dve.nop(nofuse=True)
                    if a1 and i < 2:
                        x_stats(L + 2, 2 * i, h)
                    qkv_rest(i)
                    mean(i)
                    if a1:
                        if i < 2:
                            x_stats(L + 2, 2 * i + 1, h)
                        rest(k + i + 2, (i + 2) % GT)
                        if i == 2:
                            x_moments(L + 2, h)

            for h in range(2):
                dve.wait_ge(s_ld[h], 16)
                for i in range(GT):
                    x_stats(h, i, h)
                x_moments(h, h)
            rest(0, 0)
            rest(1, 1)
            with dve.Fori(0, GB // 2) as g:
                for h in range(2):
                    body(g * 2 + h, h, True, False)
            with dve.Fori(1, B) as step:
                energy(step)
                with dve.Fori(0, GB // 2) as g:
                    for h in range(2):
                        body(step * GB + g * 2 + h, h, True, True)
            energy(B)
            with dve.Fori(0, GB) as g:
                body(g + B * GB, 0, False, True)

            chain = Chain(dve, s_dve)
            V = nc.vector
            A, Bw, Cw, Dw = work_a[:, :], work_b, work_c, work_d
            G = gates[:, :]

            def tiles(a):
                return a.rearrange("p (k j) -> p k j", j=X)

            def rows_(a):
                return a.unsqueeze(2).to_broadcast([P, K, X])

            def sums(a):
                return V.tensor_reduce(part[:, :].rearrange("p (b j) -> p b j", b=B),
                                       a.rearrange("p (b t j) -> p b j t", b=B, j=X), AX.X, ALU.add)

            total = bank[0][:, 0:BX]

            dve.wait_ge(s_sd, NG + 2)
            dve.wait_ge(s_r1, NG + 1)
            dve.wait_ge(s_const2, 5)
            chain(V.tensor_tensor(tiles(A), lg[:, 0:K, 0:X], rows_(sd0[:, 0:K]), ALU.mult))
            chain(V.scalar_tensor_tensor(tiles(A), lg[:, TB:TB + K, X:2 * X], SY * SGATE / (SQ * SLOG), tiles(A),
                                         ALU.mult, ALU.add))
            chain(V.tensor_tensor(tiles(A), tiles(A), rows_(r1[:, :]), ALU.mult))
            chain(V.tensor_scalar(G, A, 1.0 / (SY * SGATE), CLIP_EPS, ALU.mult, ALU.max))

            with dve.Fori(0, ROUNDS) as r:
                n0 = chain.n
                sums(G).then_inc(s_part, 1)
                dve.wait_ge(s_sum, r + 1)
                chain(V.reciprocal(inv[:, :], total), r * 5)
                chain(V.tensor_tensor(by_tile(G), by_tile(G), to_tiles(inv[:, :]), ALU.mult), r * 5)
                chain(V.tensor_reduce(row[:, :], tiles(G), AX.X, ALU.add), r * 5)
                chain(V.reciprocal(row_r[:, :], row[:, :]), r * 5)
                chain(V.tensor_tensor(tiles(G), tiles(G), rows_(row_r[:, :]), ALU.mult), r * 5)
                assert chain.n - n0 == 5
            chain.n += (ROUNDS - 1) * 5

            V.engine_nop().then_inc(s_gates, 1)

            T2 = 2 * BX
            junk = qT_w[0:T2, KX:KX + HT * P // 2].bitcast(F16)
            c_f = cand[0:T2].bitcast(F32)
            total1 = bank[5][0:T2, 0:1]
            chain(V.tensor_copy(cand[:, :], bits_i[:, 0:1]))
            dve.wait_ge(s_gc, 4)
            with dve.Fori(0, BITS // BB) as r:
                n0 = chain.n
                for i in range(BB):
                    V.tensor_scalar(junk, gT, c_f, 0.0, ALU.is_ge, ALU.add, accum_out=cnt[0:T2]).then_inc(s_cnt, 1)
                    b0, b1 = bass.ds(r * BB + i, 1), bass.ds(r * BB + i + 1, 1)
                    chain(V.tensor_tensor(cand_x[:, :], cand[:, :], bits_i[:, b1], ALU.bitwise_xor), r * 3 * BB)
                    dve.wait_ge(s_tot, r * BB + i + 1)
                    dve.nop(nofuse=True)
                    chain(V.tensor_scalar(fail[0:T2], total1, CAP - 0.5, bits_f[0:T2, b0], ALU.is_lt, ALU.mult), r * 3 * BB)
                    chain(V.tensor_tensor(cand[0:T2], cand_x[0:T2], fail[0:T2], ALU.bitwise_xor), r * 3 * BB)
                assert chain.n - n0 == 3 * BB
            chain.n += (BITS // BB - 1) * 3 * BB
            V.tensor_scalar(junk, gT, c_f, 0.0, ALU.is_gt, ALU.add, accum_out=cnt[0:T2]).then_inc(s_cnt, 1)
            V.tensor_scalar(spread[0:BX, 0], ones1[0:BX, :], c_f[0:BX], None, ALU.mult)
            dve.wait_ge(s_tot, BITS + 1)
            chain(V.tensor_scalar(need1[0:BX], total1[0:BX], -1.0, float(CAP), ALU.mult, ALU.add))
            V.tensor_scalar(spread[0:BX, 1], ones1[0:BX, :], need1[0:BX], None, ALU.mult).then_inc(s_cnt, 1)

            def by_row(a):
                return a.rearrange("p (b t j) -> p b j t", b=B, j=X)

            def rows3(a):
                return a.rearrange("p (b j t) -> p b j t", b=B, j=X)

            def rows2(a):
                return a.rearrange("p (r t) -> p r t", t=TB)

            def of_row(a):
                return a.unsqueeze(2).to_broadcast([P, BX, TB])

            def of_row3(a):
                return a.rearrange("p (b j) -> p b j", b=B).unsqueeze(3).to_broadcast([P, B, X, TB])

            def f16(a):
                b = a.bitcast(F16)
                return b[:, 0:KX], b[:, KX:2 * KX]

            def starts(scan):
                ends = rows2(scan)[:, :, TB - 1]
                V.tensor_copy(prev[:, 1:BX], ends[:, 0:BX - 1])
                chain(V.memset(prev[:, 0:1], 0.0))
                chain(V.tensor_tensor(part[:, :], ends, prev[:, :], ALU.subtract))
                V.engine_nop().then_inc(s_part, 1)

            (above, equal), (prefix, low), (flag, chosen) = f16(Bw), f16(Cw), f16(A)
            for j in range(X):
                V.tensor_scalar(rows3(flag)[:, :, j], by_row(G)[:, :, j], 0.5, 2.0 * (j + 1), ALU.is_gt, ALU.add)
            dve.wait_ge(s_tot, BITS + 2)
            chain(V.tensor_copy(thr_need[:, :, :], bank[5][:, 0:2 * BX].rearrange("p (a r) -> p a r", a=2)))
            chain(V.tensor_tensor(rows3(equal), by_row(G), of_row3(thr_need[:, 0]), ALU.is_equal))
            chain(V.tensor_tensor_scan(prefix, one1[:, :].to_broadcast([P, KX]), equal, 0.0, ALU.mult, ALU.add))
            starts(prefix)
            V.tensor_tensor(rows3(above), by_row(G), of_row3(thr_need[:, 0]), ALU.is_gt)
            chain(V.scalar_tensor_tensor(lim[:, :], prev[:, :], 1.0, thr_need[:, 1], ALU.add, ALU.add))
            dve.wait_ge(s_sum, ROUNDS + 1)
            chain(V.tensor_tensor(lim[:, :], lim[:, :], total, ALU.subtract))
            chain(V.tensor_tensor(rows2(low), rows2(prefix), of_row(lim[:, :]), ALU.is_lt))
            chain(V.tensor_tensor(low, low, equal, ALU.mult))
            chain(V.tensor_tensor(chosen, above, low, ALU.add))

            chain(V.tensor_tensor(chosen, chosen, flag, ALU.mult))
            chain(V.tensor_reduce(m_max[:, :].rearrange("p (b t) -> p b t", b=B),
                                  chosen.rearrange("p (b j t) -> p b t j", b=B, j=X), AX.X, ALU.max))
            active, prefix = f16(Bw)
            for j in range(X):
                ins = V.tensor_scalar(rows3(active)[:, :, j], m_max[:, :].rearrange("p (b t) -> p b t", b=B),
                                      2.0 * (j + 1) + 1.0, None, ALU.is_equal)
            chain(ins)

            chain(V.tensor_tensor_scan(prefix, one1[:, :].to_broadcast([P, KX]), active, 0.0, ALU.mult, ALU.add))
            starts(prefix)
            dve.wait_ge(s_sum, ROUNDS + 2)
            counts = bank[0][:, BX:2 * BX].rearrange("p (b j) -> p j b", b=B)

            def xb(a):
                return a[:, :].rearrange("p (j b) -> p j b", j=X)

            V.tensor_reduce(tot[:, :], counts, AX.X, ALU.add)
            chain(V.tensor_copy(xb(sel), counts))
            chain(V.tensor_tensor_scan(excl[:, :], one1[:, :].to_broadcast([P, BX]), sel[:, :], 0.0, ALU.mult, ALU.add))
            chain(V.tensor_tensor(excl[:, :], excl[:, :], sel[:, :], ALU.subtract))
            chain(V.tensor_scalar(nt_i[:, :], tot[:, :], P - 1.0, None, ALU.add))
            chain(V.tensor_single_scalar(nt_i[:, :], nt_i[:, :], 7, ALU.arith_shift_right))
            chain(V.tensor_copy(nt_f[:, :], nt_i[:, :]))
            chain(V.tensor_tensor_scan(cum[:, :], one1[:, :].to_broadcast([P, X]), nt_f[:, :], 0.0, ALU.mult, ALU.add))
            chain(V.tensor_tensor(start[:, :], cum[:, :], nt_f[:, :], ALU.subtract))
            chain(V.tensor_scalar(nq_i[:, :], cum[:, X - 1:X], 1.0, 3.0, ALU.max, ALU.add))
            V.tensor_single_scalar(nq_i[:, :], nq_i[:, :], 2, ALU.arith_shift_right).then_inc(s_table, 1)
            chain(V.scalar_tensor_tensor(corr[:, :], start[:, :], float(P), xb(excl)[:, :, 0], ALU.mult, ALU.subtract))
            chain(V.tensor_tensor(xb(base_i), xb(excl), corr[:, :].unsqueeze(2).to_broadcast([P, X, B]), ALU.add))
            V.tensor_single_scalar(tile_i[:, :], base_i[:, :], 7, ALU.arith_shift_right)
            chain(V.tensor_single_scalar(off_i[:, :], base_i[:, :], P - 1, ALU.bitwise_and))
            V.tensor_copy(tile_f[:, :], tile_i[:, :])
            chain(V.tensor_tensor(xb(off_f), xb(off_i), win_x[:, :].unsqueeze(2).to_broadcast([P, X, B]), ALU.add))
            chain(V.tensor_tensor(lim[:, :], bank[0][:, 0:BX], prev[:, :], ALU.subtract))
            chain(V.tensor_tensor(lim[:, :].rearrange("p (b j) -> p j b", b=B), lim[:, :].rearrange("p (b j) -> p j b", b=B),
                                  xb(off_f), ALU.add))
            places = A
            chain(V.tensor_tensor(rows2(places), rows2(prefix), of_row(lim[:, :]), ALU.add))
            chain(V.tensor_tensor(places, places, active, ALU.mult))
            chain(V.tensor_reduce(row[:, :].rearrange("p (b t) -> p b t", b=B),
                                  places.rearrange("p (b j t) -> p b t j", b=B, j=X), AX.X, ALU.add))
            chain(V.tensor_scalar(pos_i[:, :], row[:, :], -1.0, None, ALU.add))
            V.tensor_single_scalar(lo_i[:, :], pos_i[:, :], P - 1, ALU.bitwise_and)
            chain(V.tensor_single_scalar(hi_i[:, :], pos_i[:, :], 7, ALU.arith_shift_right))
            V.tensor_copy(lo16[:, :], lo_i[:, :])
            chain(V.tensor_copy(hi16[:, :], hi_i[:, :]))

            dve.sem_inc(s_list, 2)
            with dve.Fori(0, B) as b:
                for h in range(2):
                    n0 = chain.n
                    tiles_h = bass.ds((b * 2 + h) * HT, HT)
                    dve.wait_ge(s_list, b * 2 + h + 1)
                    dve.nop(nofuse=True)
                    V.tensor_tensor(eq_w[:, h], iota_c[:, :, :], hi16[:, tiles_h].unsqueeze(1).to_broadcast([P, WX, HT]),
                                    ALU.is_equal).then_inc(s_eq, 1)
                    V.tensor_tensor(oh_l[:, h], iota_l, lo16[:, tiles_h].unsqueeze(1).to_broadcast([P, P, HT]), ALU.is_equal)
                    dve.wait_ge(s_eq, b * 2 + h + 1)
                    V.tensor_tensor(oh_w[:, h, 1], eq_w[:, h], tok_b[:, h * HT:(h + 1) * HT].unsqueeze(1).to_broadcast([P, WX, HT]),
                                    ALU.mult).then_inc(s_oh, 1)

            chain(V.memset(et_f[:, 0], 0.0))
            for j in range(1, X):
                chain(V.scalar_tensor_tensor(et_f[:, j % 2], iota_t[:, :], start[:, j:j + 1], et_f[:, (j + 1) % 2],
                                             ALU.is_ge, ALU.add))
            V.tensor_copy(et_i[:, :], et_f[:, (X - 1) % 2]).then_inc(s_table, 1)

            chain(V.tensor_tensor(mask[:, :], mask_a[:, :], mask_b[:, :], ALU.add))
            chain(V.scalar_tensor_tensor(win_f[:, :], mask_b[:, :], -float(WX), win_f[:, :], ALU.mult, ALU.add))
            chain(V.tensor_tensor(win_f[:, :], win_f[:, :], mask[:, :], ALU.mult))
            chain(V.tensor_reduce(win_s[:, :], win_f[:, :], AX.X, ALU.add))
            chain(V.scalar_tensor_tensor(mask_b[:, :], mask_a[:, :], float(TB), mask_b[:, :], ALU.mult, ALU.add))
            chain(V.tensor_reduce(scale_s[:, :], mask_b[:, :], AX.X, ALU.add))
            chain(V.tensor_tensor(xb(sel), xb(tile_f), mask[:, :].unsqueeze(2).to_broadcast([P, X, B]), ALU.mult))
            chain(V.tensor_reduce(dest[:, :], sel[:, :].rearrange("p (j b) -> p b j", j=X), AX.X, ALU.add))
            chain(V.tensor_scalar(dest[:, :], dest[:, :], win_s[:, :], None, ALU.add))
            for b in range(B):
                ins = V.tensor_scalar(oh_t[:, b], iota_t[:, :], dest[:, b:b + 1], scale_s[:, :], ALU.is_equal, ALU.mult)
            ins.then_inc(s_dest, 1)
            dve.wait_ge(s_tab, 1)
            chain(V.tensor_scalar(empty[:, :], bank[2][:, 0:TABLE], 0.0, EMPTY + 1.0, ALU.is_equal, ALU.mult))
            V.scalar_tensor_tensor(table[:, :], bank[2][:, 0:TABLE], -1.0, empty[:, :], ALU.add, ALU.add).then_inc(s_table, 1)

            dve.wait_ge(s_table, 3)
            nq = dve.value_load(nq_i[0:1, 0:1], min_val=1, max_val=TILES // 4)

            def row_stats(n, j, r):
                i = j % 4
                dve.wait_ge(s_ga[j], r * 16 + 16)
                dve.nop(nofuse=True)
                V.bn_stats(stats[:, 0, i], xg[:, j]).then_inc(s_fbn, 1)
                dve.wait_ge(s_fbn, n + 1)
                dve.nop(nofuse=True)
                V.bn_aggr(mv[:, 0, i], stats[:, 0, i]).then_inc(s_fmv, 1)

            def row_var(n, i):
                dve.wait_ge(s_fmv, n + 1)
                V.tensor_scalar(vpe[:, i:i + 1], mv[:, 0, i, 1:2], LN_EPS, SY ** -2, ALU.add, ALU.mult).then_inc(s_fvar, 1)

            def row_y(n, j):
                i = j % 4
                dve.wait_ge(s_frs, n + 1)
                V.tensor_scalar(y0[:, i], xg[:, j], mv[:, 0, i, 0:1], rstd[:, i:i + 1], ALU.subtract, ALU.mult).then_inc(s_fy, 1)

            def row_rest(i, n):
                dve.wait_ge(s_fhi, n + 1)
                V.tensor_tensor(y_lo[:, i], p_xT[i % 2][:, :], y_hi[:, i], ALU.subtract).then_inc(s_flo, 1)

            for i in range(4):
                row_stats(i, i, 0)
                row_var(i, i)
            for i in range(3):
                row_y(i, i)
            row_rest(0, 0)
            row_rest(1, 1)
            with dve.Fori(0, -(-TILES // AHEAD)) as r:
                for h in range(2):
                    with dve.If(r * 2 + h < nq):
                        for i in range(4):
                            n = r * AHEAD + h * 4 + i
                            row_stats(n + 4, (h * 4 + i + 4) % AHEAD, r + h)
                            row_y(n + 3, (h * 4 + i + 3) % AHEAD)
                            row_var(n + 4, i)
                            row_rest((i + 2) % 4, n + 2)
                            dve.wait_ge(s_sc[i], (r * 2 + h + 1) * 16)
                            dve.wait_ge(s_fmm, n + 1)
                            V.scalar_tensor_tensor(yo[:, i], p_out[i % 2][:, :], 1.0 / (SY * SX), xg[:, h * 4 + i],
                                                   ALU.mult, ALU.add).then_inc(s_fin, 1)
                    with dve.Else():
                        dve.nop()
                    dve.nop()

        @block.tensor
        def _(pe):
            pe.sem_inc(s_lo, 2)
            pe.sem_inc(s_ql, 2)
            pe.sem_inc(s_qc, 1)
            pe.sem_inc(s_x1, 2)
            pe.sem_inc(s_fin, 2)
            pe.wait_ge(s_const, 2)
            pe.wait_ge(s_w, 16 * 6)
            for h in range(2):
                for c in range(2):
                    for m in range(3):
                        ins = nc.tensor.transpose(bank[h][:, c * 3 * D + m * D:c * 3 * D + (m + 1) * D],
                                                  wall[:, m, (2 * h + c) * P:(2 * h + c + 1) * P], ident[0:D, 0:D])
                ins.then_inc(s_setup_pe, 1)
            for c in range(CH):
                ins = nc.tensor.transpose(bank[2][:, c * P:(c + 1) * P], wod[:, c].rearrange("p r d -> p (r d)"),
                                          ident[:, :])
            ins.then_inc(s_setup_pe, 1)
            for c in range(CH):
                ins = nc.tensor.matmul(bank[3][:, 0:X], inv_e[:, :], gw[:, c], start=c == 0, stop=c == CH - 1)
            ins.then_inc(s_setup_pe, 1)
            pe.wait_ge(s_setup_v, 3)
            for c in range(CH):
                ins = nc.tensor.matmul(bank[4][:, 0:X], wod[:, c].rearrange("p r d -> p (r d)"), gwc[:, c],
                                       start=c == 0, stop=c == CH - 1)
            ins.then_inc(s_setup_pe, 1)
            pe.wait_ge(s_setup_a, 5)

            def zero_energy(start):
                return nc.tensor.matmul(p_en[:, 0:P], zero16[:, :], zero16[:, :], start=start, stop=not start)

            def energy(step):
                pe.wait_ge(s_ec, step * 2)
                pe.wait_ge(s_x1, (step - 1) * TB + 2)
                for a in range(2):
                    nc.tensor.matmul(p_out[0][:, :], en[:, a].rearrange("p r d -> p (r d)"), woT[:, 0:E],
                                     start=a == 0, stop=a == 1)
                for a in range(2):
                    ins = nc.tensor.matmul(p_out[1][:, 0:X], en[:, a].rearrange("p r d -> p (r d)"), woT[:, E:E + X],
                                           start=a == 0, stop=a == 1)
                ins.then_inc(s_g, 1)
                pe.wait_ge(s_gl, step)

            def transpose(n, i):
                pe.wait_ge(s_y, n + 1)
                for c in range(CH):
                    ins = nc.tensor.transpose(p_xT[i % 2][:, c * P:(c + 1) * P], y0[:, i, c * P:(c + 1) * P],
                                              ident[:, :])
                ins.then_inc(s_T, 1)

            def body(L, a1, a2):
                k = L * GT
                M = L - GB
                m = M * GT

                def attend(i):
                    if a2:
                        pe.wait_ge(s_x1, m + i + 1)
                        pe.nop(nofuse=True)
                        for g, first in ((g_hi, True), (g_lo, False)):
                            ins = nc.tensor.matmul(p_out[i % 2][:, :], qT[:, M % RING, i], g[:, 0:E],
                                                   start=first, stop=not first)
                        ins.then_inc(s_o, 1)

                def project(i):
                    pe.wait_ge(s_ql, k + i + 1)
                    pe.nop(nofuse=True)
                    if a1:
                        pe.wait_ge(s_lo, k + i + 3)
                        for c in range(CH):
                            f = slice(c * P, (c + 1) * P)
                            nc.tensor.matmul(p_qkv[i % 2][:, 0:NC], y_hi[:, i, f], w_hi[:, c], start=c == 0, stop=False)
                            nc.tensor.matmul(p_qkv[i % 2][:, 0:NC], y_hi[:, i, f], w_lo[:, c], start=False, stop=False)
                            ins = nc.tensor.matmul(p_qkv[i % 2][:, 0:NC], y_lo[:, i, f], w_hi[:, c], start=False,
                                                   stop=c == CH - 1)
                    if a2:
                        for g, first in ((g_hi, True), (g_lo, False)):
                            ins = nc.tensor.matmul(p_qkv[i % 2][:, NC:NC + X], qT[:, M % RING, i], g[:, E:E + X],
                                                   start=first, stop=not first)
                    ins.then_inc(s_qkv, 1)

                def energy_and_qT(i):
                    if a1:
                        pe.wait_ge(s_ql, k + i + 3)
                        pe.wait_ge(s_qc, k + i + 1)
                        nc.tensor.transpose(p_qT16, qkv[:, i, 0].rearrange("p a d -> p (a d)"), ident16[:, :])
                        nc.tensor.matmul(p_en[:, 0:P], qkv[:, i, 2].rearrange("p a d -> p (a d)"),
                                         qkv[:, i, 1].rearrange("p a d -> p (a d)"), start=False,
                                         stop=False).then_inc(s_qt, 1)

                for i in range(GT):
                    attend(i)
                    project(i)
                    if i > 0:
                        energy_and_qT(i - 1)
                    if a1:
                        transpose(k + i + 2, (i + 2) % GT)
                energy_and_qT(GT - 1)

            transpose(0, 0)
            transpose(1, 1)
            zero_energy(True)
            with pe.Fori(0, GB) as g:
                body(g, True, False)
            zero_energy(False).then_inc(s_en, 1)
            with pe.Fori(1, B) as step:
                energy(step)
                zero_energy(True)
                with pe.Fori(0, GB) as g:
                    body(step * GB + g, True, True)
                zero_energy(False).then_inc(s_en, 1)
            energy(B)
            with pe.Fori(0, GB) as g:
                body(g + B * GB, False, True)

            with pe.Fori(0, ROUNDS) as r:
                pe.wait_ge(s_part, r + 1)
                nc.tensor.matmul(bank[0][:, 0:BX], ones1[:, :], part[:, :], start=True, stop=True).then_inc(s_sum, 1)
            for t in range(HT):
                q, c = t // (HT // 4), t % (HT // 4)
                if c == 0:
                    pe.wait_ge(s_go, q + 1)
                ins = nc.tensor.transpose(bank[1 + q][0:2 * BX, c * P:(c + 1) * P], g_order[:, t].rearrange("p h b j -> p (h b j)"), ident[:, :])
                if c == HT // 4 - 1:
                    ins.then_inc(s_gt, 1)
            T2 = 2 * BX
            with pe.Fori(0, BITS + 1) as r:
                pe.wait_ge(s_cnt, r + 1)
                pe.nop(nofuse=True)
                nc.tensor.matmul(bank[5][0:T2, 0:1], pair[0:T2, 0:T2], cnt[0:T2], start=True, stop=True).then_inc(s_tot, 1)
            pe.wait_ge(s_cnt, BITS + 2)
            for a in range(2):
                ins = nc.tensor.transpose(bank[5][:, a * BX:(a + 1) * BX], spread[0:BX, a], ident[0:BX, 0:BX])
            ins.then_inc(s_tot, 1)
            pe.wait_ge(s_part, ROUNDS + 1)
            nc.tensor.matmul(bank[0][:, 0:BX], before[:, :], part[:, :], start=True, stop=True).then_inc(s_sum, 1)
            pe.wait_ge(s_part, ROUNDS + 2)
            nc.tensor.matmul(bank[0][:, 0:BX], before[:, :], part[:, :], start=True, stop=True)
            nc.tensor.matmul(bank[0][:, BX:2 * BX], ones1[:, :], part[:, :], start=True, stop=True).then_inc(s_sum, 1)

            pe.sem_inc(s_wl, 1)
            with pe.Fori(0, B) as b:
                pe.wait_ge(s_wl, b + 1)
                for h in range(2):
                    pe.wait_ge(s_oh, b * 2 + h + 1)
                    pe.wait_ge(s_ea, b * 2 + h + 1)
                    for t in range(HT):
                        ins = nc.tensor.matmul(bank[1][0:2 * WX, 0:P], oh_w[:, h, :, :, t].rearrange("p q c -> p (q c)"),
                                               oh_l[:, h, :, t], start=h == 0 and t == 0, stop=h == 1 and t == HT - 1)
                    ins.then_inc(s_list, 1)
            pe.wait_ge(s_dest, 1)
            pe.wait_ge(s_wl, B + 1)
            for b in range(B):
                ins = nc.tensor.matmul(bank[2][:, 0:TABLE], win_list[0:2 * WX, b], oh_t[0:2 * WX, b], start=b == 0,
                                       stop=b == B - 1)
            ins.then_inc(s_tab, 1)

            pe.wait_ge(s_table, 3)
            pe.wait_ge(s_el, 2 * X)
            nq = pe.value_load(nq_i[0:1, 0:1], min_val=1, max_val=TILES // 4)

            def row_transpose(i, n):
                pe.wait_ge(s_fy, n + 1)
                for c in range(CH):
                    ins = nc.tensor.transpose(p_xT[i % 2][:, c * P:(c + 1) * P], y0[:, i, c * P:(c + 1) * P], ident[:, :])
                ins.then_inc(s_fT, 1)

            row_transpose(0, 0)
            row_transpose(1, 1)
            with pe.Fori(0, -(-TILES // AHEAD)) as r:
                for h in range(2):
                    with pe.If(r * 2 + h < nq):
                        for i in range(4):
                            n = r * AHEAD + h * 4 + i
                            j = pe.value_load(et_i[0:1, bass.ts(n, 1)], min_val=0, max_val=X - 1)
                            pe.wait_ge(s_flo, n + 1)
                            pe.nop(nofuse=True)
                            row_transpose((i + 2) % 4, n + 2)
                            pe.wait_ge(s_fin, n + 1)
                            for c in range(CH):
                                f = slice(c * P, (c + 1) * P)
                                nc.tensor.matmul(p_out[i % 2][:, :], y_hi[:, i, f], e_hi[:, j, c], start=c == 0, stop=False)
                                nc.tensor.matmul(p_out[i % 2][:, :], y_hi[:, i, f], e_lo[:, j, c], start=False, stop=False)
                                ins = nc.tensor.matmul(p_out[i % 2][:, :], y_lo[:, i, f], e_hi[:, j, c], start=False,
                                                       stop=c == CH - 1)
                            ins.then_inc(s_fmm, 1)
                    with pe.Else():
                        pe.nop()
                    pe.nop()


_INS = ["L0_attn_x", "L0_attn_wq", "L0_attn_wk", "L0_attn_wv", "L0_attn_wo", "L0_ffn_gate_w", "L0_ffn_experts"]


def kernel(**inputs):
    import numpy as _np
    import concourse.bacc as _bacc
    from concourse import mybir as _mybir
    from concourse.bass_utils import run_bass_kernel_spmd as _run

    nc = _bacc.Bacc("TRN2", target_bir_lowering=False, num_devices=1)
    arrays, args = {}, []
    for name in _INS:
        a = _np.ascontiguousarray(inputs[name])
        arrays[f"in_{name}_dram"] = a
        args.append(nc.dram_tensor(f"in_{name}_dram", a.shape, _mybir.dt.from_np(a.dtype), kind="ExternalInput").ap())
    shape = inputs["L0_attn_x"].shape
    args.append(nc.dram_tensor("out_0_dram", shape, _mybir.dt.float32, kind="ExternalOutput").ap())
    linear_attention_moe_kernel(nc, *args)
    r = _run(nc, [arrays], core_ids=[0])
    return r.results[0]["out_0_dram"]
```

```python
from contextlib import ExitStack


def linear_attention_moe_kernel(nc, x, wq, wk, wv, wo, gate_w, experts, out):
    import concourse.bass as bass
    from concourse import mybir

    F32, F16, I32 = mybir.dt.float32, mybir.dt.float16, mybir.dt.int32
    ALU, ACT, AX = mybir.AluOpType, mybir.ActivationFunctionType, mybir.AxisListType

    P = 128
    B, N, E = x.shape
    D = wq.shape[0]
    X = experts.shape[0]
    CH = E // P
    TB = N // P
    K = B * TB
    GT = 4
    GB = TB // GT
    NG = B * GB
    RING = GB + 4
    CAP = N // X
    LN_EPS, CLIP_EPS, ITERS = 1e-5, 1e-6, 8
    OUT_SCALE = (3.0 / D) ** 0.5

    SY, SW, SQ, SGATE, SLOG, SX = 64.0, 256.0, 64.0, 16.0, 1.0 / 16, 16.0
    NC = 3 * D + X
    RB = 6
    AHEAD = 8
    TILES = -(-(K + X) // (RB * AHEAD)) * RB * AHEAD
    TABLE = TILES + AHEAD
    WIN = CAP // P + 1
    WX = WIN * X
    HT = TB // 2
    ROUNDS, SB = ITERS, 4
    BITS, BB = 30, 6
    HUGE = 2.0 ** 100
    EMPTY = float(1 << 20)

    ctx = ExitStack()
    with ctx:
        def sb(name, shape, dt):
            return ctx.enter_context(nc.sbuf_tensor(name, shape, dt))

        def pb(name, shape, dt):
            return ctx.enter_context(nc.psum_tensor(name, shape, dt))

        def sem(name):
            return ctx.enter_context(nc.semaphore(name))

        big = sb("big", [P, RING * GT * E], F32)
        xr = big[:, :].rearrange("p (l t e) -> p l t e", l=RING, t=GT)
        HE = X * CH * E // 2
        e_hi = big[:, 0:HE].bitcast(F16).rearrange("p (x c n) -> p x c n", x=X, c=CH)
        e_lo = big[:, HE:2 * HE].bitcast(F16).rearrange("p (x c n) -> p x c n", x=X, c=CH)
        half = 2 * HE
        e_f = big[:, half:half + HE].rearrange("p (x c n) -> p x c n", x=X // 2, c=CH)
        xg = big[:, half:half + AHEAD * E].rearrange("p (i e) -> p i e", i=AHEAD)
        yo = big[:, half + AHEAD * E:half + (AHEAD + 4) * E].rearrange("p (i e) -> p i e", i=4)

        qT_w = sb("qT", [P, max(2 * K * X, RING * GT * P // 2)], F32)
        qT = qT_w[:, 0:RING * GT * P // 2].bitcast(F16).rearrange("p (l t n) -> p l t n", l=RING, t=GT)
        y0 = sb("y0", [P, GT, E], F32)
        y_w = sb("y_pair", [P, GT * E], F32)
        y_hi = y_w[:, 0:GT * E // 2].bitcast(F16).rearrange("p (i e) -> p i e", i=GT)
        y_lo = y_w[:, GT * E // 2:].bitcast(F16).rearrange("p (i e) -> p i e", i=GT)
        qkv = sb("qkv", [P, GT, 3, 2, D], F16)
        w_hi = sb("w_hi", [P, CH, NC], F16)
        w_lo = sb("w_lo", [P, CH, NC], F16)
        woT = sb("woT", [P, E + X], F32)
        en = sb("en", [P, 2, D], F32)
        en_half = sb("en_half", [P, D], F32)
        g_hi = sb("g_hi", [P, E + X], F16)
        g_lo = sb("g_lo", [P, E + X], F16)
        ident = sb("ident", [P, P], F32)
        ident16 = sb("ident16", [P, P], F16)
        zero16 = sb("zero16", [P, P], F16)
        stats = sb("stats", [P, 2, GT, 6], F32)
        mv = sb("mv", [P, 2, GT, 2], F32)
        sum1 = sb("sum1", [P, GT], F32)
        nmean1 = sb("nmean1", [P, GT], F32)
        ssq1 = sb("ssq1", [P, GT], F32)
        vpe1 = sb("vpe1", [P, GT], F32)
        squares = sb("squares", [P, GT, E], F16)
        vpe = sb("vpe", [P, GT], F32)
        rstd = sb("rstd", [P, GT], F32)
        rs = sb("rs", [P, 2, GT], F32)
        nm = sb("nm", [P, GT], F32)
        nmr = sb("nmr", [P, 2, GT], F32)
        mhalf = sb("mhalf", [P, GT], F32)
        LG = max(K + TB, (2 * P + 6 * WX) * HT // (4 * X) + 1)
        lg = sb("lg", [P, LG, 2 * X], F32)

        bank = [pb(f"bank{i}", [P, 512], F32) for i in range(8)]
        p_xT, p_qkv, p_out, p_en, p_qT = bank[0:2], bank[2:4], bank[4:6], bank[6], bank[7]
        p_qT16 = p_qT[:, 0:P // 2].bitcast(F16)

        sd = big[:, 2 * GT * E:]
        wall = sd[0:D, 0:3 * E].rearrange("p (m e) -> p m e", m=3)
        wod = sd[:, 3 * E:4 * E].rearrange("p (c r d) -> p c r d", c=CH, r=2)
        gw = sd[:, 4 * E:4 * E + CH * X].rearrange("p (c j) -> p c j", c=CH)
        gwc = sd[:, 5 * E:5 * E + CH * X].rearrange("p (c j) -> p c j", c=CH)
        inv_e = sb("inv_e", [P, P], F32)

        BX, KX = B * X, K * X
        gates = sb("gates", [P, KX], F32)
        work_a = sb("work_a", [P, KX], F32)
        work_b, work_c = qT_w[:, 0:KX], qT_w[:, KX:2 * KX]
        g_halves = gates[:, :].rearrange("p (b h t j) -> p h t b j", b=B, h=2, t=HT)
        g_order = work_a[:, :].rearrange("p (t h b j) -> p t h b j", t=HT, h=2, b=B)
        gT = y_w[0:2 * BX, 0:HT * P]
        sd0 = sb("sd0", [P, K + 2 * GT], F32)
        r1 = sb("r1", [P, K], F32)
        row = sb("row", [P, K], F32)
        row_r = sb("row_r", [P, K], F32)
        m_max = sb("m_max", [P, K], F16)
        pos_i = sb("pos_i", [P, K], I32)
        lo_i = sb("lo_i", [P, K], I32)
        hi_i = sb("hi_i", [P, K], I32)
        lo16 = sb("lo16", [P, K], F16)
        hi16 = sb("hi16", [P, K], F16)
        tok_a = sb("tok_a", [P, B], F32)
        tok_b = sb("tok_b", [P, TB], F16)
        part = sb("part", [P, BX], F32)
        inv = sb("inv", [P, BX], F32)
        pair = sb("pair", [P, P], F32)
        bits_f = sb("bits_f", [P, BITS + 1], F32)
        bits_i = sb("bits_i", [P, BITS + 1], I32)
        cand = sb("cand", [P, 1], I32)
        bits_2f = sb("bits_2f", [P, BITS], F32)
        bits_2 = sb("bits_2", [P, BITS], I32)
        cand_up = sb("cand_up", [P, 1], I32)
        cand_down = sb("cand_down", [P, 1], I32)
        cnt = sb("cnt", [P, 1], F32)
        need1 = sb("need1", [P, 1], F32)
        spread = sb("spread", [P, 2, P], F32)
        thr_need = sb("thr_need", [P, 2, BX], F32)
        prev = sb("prev", [P, BX], F32)
        excl = sb("excl", [P, BX], F32)
        base_i = sb("base_i", [P, BX], I32)
        tile_i = sb("tile_i", [P, BX], I32)
        off_i = sb("off_i", [P, BX], I32)
        tile_f = sb("tile_f", [P, BX], F32)
        off_f = sb("off_f", [P, BX], F32)
        need = sb("need", [P, BX], F32)
        lim = sb("lim", [P, BX], F32)
        win_x = sb("win_x", [P, X], F32)
        one1 = sb("one1", [P, 1], F32)
        ones1 = sb("ones1", [P, P], F32)
        before = sb("before", [P, P], F32)
        tot = sb("tot", [P, X], F32)
        nt_f = sb("nt_f", [P, X], F32)
        nt_i = sb("nt_i", [P, X], I32)
        cum = sb("cum", [P, X], F32)
        start = sb("start", [P, X], F32)
        corr = sb("corr", [P, X], F32)
        nq_f = sb("nq_f", [P, 1], F32)
        nq_i = sb("nq_i", [P, 1], I32)
        iota_t = sb("iota_t", [P, TABLE], F16)
        iota_l = squares[:, :, :].rearrange("p i e -> p (i e)")[:, 0:P * HT].rearrange("p (l t) -> p l t", l=P)
        iota_c = sb("iota_c", [P, WX, HT], F16)
        mask_a = sb("mask_a", [P, X], F32)
        mask_b = sb("mask_b", [P, X], F32)
        mask = sb("mask", [P, X], F32)
        win_f = sb("win_f", [P, X], F32)
        win_s = sb("win_s", [P, 1], F32)
        scale_s = sb("scale_s", [P, 1], F32)
        sel = sb("sel", [P, X * B], F32)
        dest = sb("dest", [P, B], F32)
        et_f = sb("et_f", [P, 2, TABLE], F32)
        et_c = sb("et_c", [P, TABLE], F32)
        et_i = sb("et_i", [P, TABLE], I32)
        empty = sb("empty", [P, TABLE], F32)
        table = sb("table", [P, TABLE], I32)
        lg16 = lg[:, :, :].rearrange("p k j -> p (k j)").bitcast(F16)
        oh_l = lg16[:, 0:2 * P * HT].rearrange("p (h l t) -> p h l t", h=2, l=P)
        oh_w = lg16[:, 2 * P * HT:2 * P * HT + 4 * WX * HT].rearrange("p (h q c t) -> p h q c t", h=2, q=2, c=WX)
        eq_w = lg16[:, 2 * P * HT + 4 * WX * HT:2 * P * HT + 6 * WX * HT].rearrange("p (h c t) -> p h c t", h=2, c=WX)
        win_list = sb("win_list", [P, B, P], F16)
        oh_t = work_c[:, 0:B * TABLE // 2].bitcast(F16).rearrange("p (b n) -> p b n", b=B)
        idx_g = sb("idx_g", [P, AHEAD], I32)
        idx_s = sb("idx_s", [P, GT], I32)

        x_v = x.rearrange("b (p g t) e -> b g p t e", p=P, t=GT)
        o_v = out.rearrange("b (p g t) e -> b g p t e", p=P, t=GT)

        s_w = sem("weights_loaded")
        s_const = sem("constants_made")
        s_setup_pe = sem("setup_products_done")
        s_setup_a = sem("setup_high_parts_done")
        s_setup_v = sem("setup_rests_done")
        s_ld = [sem(f"x_loaded{i}") for i in range(2)]
        s_st = [sem(f"x1_stored{i}") for i in range(2)]
        s_bn = sem("x_stats_done")
        s_mv = sem("x_moments_done")
        s_pool = sem("pool_chain")
        s_rs = sem("x_rstd_done")
        s_y = sem("y_done")
        s_T = sem("y_transposed")
        s_hi = sem("y_high_part_done")
        s_lo = sem("y_rest_done")
        s_qkv = sem("qkv_done")
        s_qh = sem("qkv_high_part_done")
        s_ql = sem("qkv_rest_done")
        s_qt = sem("energy_and_qT_done")
        s_qc = sem("qT_copied")
        s_en = sem("energy_summed")
        s_half = sem("half_of_energy_copied")
        s_ec = sem("energy_copied")
        s_g = sem("g_product_done")
        s_gh = sem("g_high_part_done")
        s_gl = sem("g_rest_done")
        s_o = sem("attention_out_done")
        s_x1 = sem("x1_done")
        s_nm1 = sem("x1_means_done")
        s_sq = sem("x1_squares_summed")
        s_pool1 = sem("pool_chain1")
        s_r1 = sem("x1_rstd_done")

        s_ex = sem("experts_loaded")
        s_eh = sem("experts_high_part_done")
        s_el = sem("experts_rest_done")
        s_dve = sem("vector_chain")
        s_const2 = sem("constants2_made")
        s_sd = sem("deviations_done")
        s_part = sem("parts_of_sum_done")
        s_sum = sem("sum_done")
        s_gates = sem("gates_done")
        s_go = sem("gates_ordered")
        s_gt = sem("gates_transposed")
        s_gc = sem("gates_copied")
        s_cnt = sem("count_parts_done")
        s_tot = sem("count_done")
        s_eq = sem("window_one_hots_done")
        s_ea = sem("window_one_hots_scaled")
        s_oh = sem("one_hots_done")
        s_list = sem("one_hots_summed")
        s_wl = sem("window_list_copied")
        s_place = sem("places_done")
        s_et = sem("experts_of_tiles_chain")
        s_dest = sem("places_of_windows_done")
        s_tab = sem("table_summed")
        s_table = sem("table_done")
        s_zero = sem("gather_places_zeroed")
        s_ga = [sem(f"gathered{i}") for i in range(AHEAD)]
        s_sc = [sem(f"scattered{i}") for i in range(4)]
        s_fbn = sem("row_stats_done")
        s_fmv = sem("row_moments_done")
        s_fvar = sem("row_variance_done")
        s_frs = sem("row_rstd_done")
        s_fy = sem("row_y_done")
        s_fT = sem("row_y_transposed")
        s_fhi = sem("row_high_part_done")
        s_flo = sem("row_rest_done")
        s_fmm = sem("row_product_done")
        s_fin = sem("row_sum_done")
        s_idx = sem("indices_copied")

        class Chain:

            def __init__(self, eng, sem):
                self.eng, self.sem, self.n = eng, sem, 0

            def __call__(self, ins, rounds=0):
                self.n += 1
                ins.then_inc(self.sem, 1)
                self.eng.wait_ge(self.sem, rounds + self.n)
                self.eng.nop(nofuse=True)

        def by_tile(a):
            return a.rearrange("p (b t j) -> p b t j", b=B, j=X)

        def to_tiles(a):
            return a.rearrange("p (b j) -> p b j", b=B).unsqueeze(2).to_broadcast([P, B, TB, X])

        block = ctx.enter_context(nc.Block())


        @block.sync
        def _(sp):
            for m, w in enumerate((wq, wk, wv)):
                sp.dma_start(wall[:, m], w).then_inc(s_w, 16)
            for r in range(2):
                sp.dma_start(wod[:, :, r], wo.rearrange("(c p) d -> p c d", p=P)).then_inc(s_w, 16)
            sp.dma_start(gw, gate_w[0].rearrange("(c p) j -> p c j", p=P)).then_inc(s_w, 16)

            def load(L, i):
                sp.dma_start(xr[:, L % RING], x_v[L // GB, L % GB]).then_inc(s_ld[i], 16)

            def store(L, i):
                sp.wait_ge(s_x1, L * GT + GT + 2)
                sp.nop(nofuse=True)
                sp.dma_start(o_v[L // GB, L % GB], xr[:, L % RING]).then_inc(s_st[i], 16)
                sp.wait_ge(s_sq, L * GT + GT * 2)
                sp.nop(nofuse=True)

            load(0, 0)
            load(1, 1)
            sp.wait_ge(s_setup_pe, 5)
            sp.wait_ge(s_setup_v, 3)
            with sp.Fori(1, RING // 2) as j:
                for i in range(2):
                    sp.wait_ge(s_bn, (j * 2 + i - 1) * GT)
                    sp.nop(nofuse=True)
                    load(j * 2 + i, i)
            with sp.Fori(RING // 2, NG // 2) as j:
                for i in range(2):
                    store((j - RING // 2) * 2 + i, i)
                    sp.wait_ge(s_st[i], (j - RING // 2 + 1) * 16)
                    sp.nop(nofuse=True)
                    sp.wait_ge(s_bn, (j * 2 + i - 1) * GT)
                    sp.nop(nofuse=True)
                    load(j * 2 + i, i)
            for i in range(2):
                sp.wait_ge(s_bn, (NG - 1 + i) * GT)
                sp.nop(nofuse=True)
                sp.sem_inc(s_ld[i], 16)
            with sp.Fori((NG - RING) // 2, NG // 2) as j:
                for i in range(2):
                    store(j * 2 + i, i)
                    sp.wait_ge(s_st[i], (j + 1) * 16)
                    sp.nop(nofuse=True)
            sp.wait_ge(s_mv, (NG + 2) * GT)
            sp.wait_ge(s_y, K + 3)
            ex_v = experts.rearrange("x (c p) n -> p x c n", p=P)
            sp.dma_start(e_f, ex_v[:, 0:X // 2]).then_inc(s_ex, 16)
            sp.wait_ge(s_el, X)
            sp.dma_start(e_f, ex_v[:, X // 2:X]).then_inc(s_ex, 16)

        @block.gpsimd
        def _(pool):
            count = [0]

            def link(ins):
                count[0] += 1
                ins.then_inc(s_pool, 1)
                pool.wait_ge(s_pool, count[0])

            nc.gpsimd.memset(mhalf[:, :], -0.5)
            nc.gpsimd.memset(zero16[:, :], 0.0)
            nc.gpsimd.memset(inv_e[:, :], 1.0 / E)
            nc.gpsimd.memset(ident16[:, :], 0.0)
            link(nc.gpsimd.memset(ident[:, :], 0.0))
            for m in (ident, ident16):
                pool.affine_select(out=m[:, :], in_=m[:, :], compare_op=ALU.not_equal, fill=1.0, base=0,
                                   pattern=[[-1, P]], channel_multiplier=1).then_inc(s_const, 1)

            def rstd_of_group(L, h, first=False):
                pool.wait_ge(s_mv, (L + 1) * GT)
                pool.nop(nofuse=True)
                if not first:
                    pool.wait_ge(s_y, (L - 1) * GT)
                    pool.wait_ge(s_sd, L)
                    pool.nop(nofuse=True)
                nc.gpsimd.tensor_scalar(vpe[:, :], mv[:, h, :, 1], LN_EPS, SY ** -2, ALU.add, ALU.mult).then_inc(s_pool, 1)
                nc.gpsimd.tensor_scalar(nm[:, :], mv[:, h, :, 0], -1.0, None, ALU.mult).then_inc(s_pool, 1)
                pool.wait_ge(s_pool, L * 3 + (count[0] + 2))
                pool.nop(nofuse=True)
                nc.gpsimd.tensor_tensor(rs[:, h], vpe[:, :], mhalf[:, :], ALU.pow).then_inc(s_pool, 1)
                pool.wait_ge(s_pool, L * 3 + (count[0] + 3))
                pool.nop(nofuse=True)
                nc.gpsimd.tensor_tensor(nmr[:, h], nm[:, :], rs[:, h], ALU.mult).then_inc(s_rs, 1)
                nc.gpsimd.tensor_tensor(sd0[:, bass.ts(L, GT)], vpe[:, :], rs[:, h], ALU.mult).then_inc(s_sd, 1)

            def rstd1_of_group(M):
                pool.wait_ge(s_sq, (M + 2) * GT)
                pool.wait_ge(s_r1, M + 1)
                pool.nop(nofuse=True)
                nc.gpsimd.tensor_scalar(vpe1[:, :], ssq1[:, :], 1.0 / E, LN_EPS, ALU.mult, ALU.add).then_inc(s_pool1, 1)
                pool.wait_ge(s_pool1, M + 1)
                pool.nop(nofuse=True)
                nc.gpsimd.tensor_tensor(r1[:, bass.ts(M, GT)], vpe1[:, :], mhalf[:, :], ALU.pow).then_inc(s_r1, 1)

            nc.gpsimd.memset(one1[:, :], 1.0)
            nc.gpsimd.memset(ones1[:, :], 1.0)
            I = dict(allow_small_or_imprecise_dtypes=True)
            nc.gpsimd.iota(win_x[:, :], [[P * WIN, X]], base=0, channel_multiplier=0, **I)
            nc.gpsimd.iota(iota_t[:, :], [[1, TABLE]], base=0, channel_multiplier=0, **I)
            nc.gpsimd.iota(iota_c[:, :, :], [[1, WX], [0, HT]], base=0, channel_multiplier=0, **I)
            nc.gpsimd.iota(tok_a[:, :], [[P, B]], base=0, channel_multiplier=1, **I)
            nc.gpsimd.iota(tok_b[:, :], [[1, TB]], base=1, channel_multiplier=0, **I)
            nc.gpsimd.iota(win_f[:, :], [[-WIN, X]], base=0, channel_multiplier=1, **I)
            for r in range(BITS):
                nc.gpsimd.memset(bits_f[:, r:r + 1], float(1 << (BITS - 1 - r)))
                nc.gpsimd.memset(bits_2f[:, r:r + 1], float((1 << (BITS - 1 - r)) | (1 << (BITS - 1 - r)) // 2))
            nc.gpsimd.memset(bits_f[:, BITS:BITS + 1], 0.0)
            nc.gpsimd.memset(mask_a[:, :], 1.0)
            nc.gpsimd.memset(mask_b[:, :], 1.0)
            nc.gpsimd.memset(pair[:, :], 0.0)
            nc.gpsimd.memset(before[:, :], 1.0).then_inc(s_const2, 1)
            pool.wait_ge(s_const2, 1)
            pool.affine_select(out=before[:, :], in_=before[:, :], compare_op=ALU.is_gt, fill=0.0, base=0,
                               pattern=[[1, P]], channel_multiplier=-1)
            for q, m in enumerate((mask_a, mask_b)):
                pool.affine_select(out=m[:, :], in_=m[:, :], compare_op=ALU.is_ge, fill=0.0, base=-q * WX,
                                   pattern=[[-WIN, X]], channel_multiplier=1)
            nc.gpsimd.tensor_copy(bits_i[:, :], bits_f[:, :])
            nc.gpsimd.tensor_copy(bits_2[:, :], bits_2f[:, :])
            pool.affine_select(out=pair[:, :], in_=pair[:, :], compare_op=ALU.not_equal, fill=HUGE, base=0,
                               pattern=[[-1, P]], channel_multiplier=1).then_inc(s_const2, 1)
            pool.wait_ge(s_const2, 2)
            for q, m in enumerate((mask_a, mask_b)):
                pool.affine_select(out=m[:, :], in_=m[:, :], compare_op=ALU.is_ge, fill=0.0, base=q * WX + WIN - 1,
                                   pattern=[[WIN, X]], channel_multiplier=-1)
            pool.affine_select(out=pair[:, :], in_=pair[:, :], compare_op=ALU.not_equal, fill=HUGE, base=BX,
                               pattern=[[-1, P]], channel_multiplier=1).then_inc(s_const2, 1)
            pool.wait_ge(s_const2, 3)
            pool.affine_select(out=pair[:, :], in_=pair[:, :], compare_op=ALU.not_equal, fill=HUGE, base=-BX,
                               pattern=[[-1, P]], channel_multiplier=1).then_inc(s_const2, 1)

            pool.sem_inc(s_r1, 1)
            rstd_of_group(0, 0, True)
            pool.wait_ge(s_sd, 1)
            rstd_of_group(1, 1, True)
            with pool.Fori(1, GB // 2 + 1) as j:
                for h in range(2):
                    rstd_of_group(j * 2 + h, h)
            with pool.Fori(GB // 2 + 1, NG // 2 + 1) as j:
                for h in range(2):
                    rstd_of_group(j * 2 + h, h)
                    rstd1_of_group(j * 2 + h - GB - 2)
            with pool.Fori(NG - GB, NG) as M:
                rstd1_of_group(M)

            nc.gpsimd.iota(iota_l, [[1, P], [0, HT]], base=0, channel_multiplier=0, **I).then_inc(s_const2, 1)

            for j in range(X):
                pool.wait_ge(s_eh, j + 1)
                f = e_f[:, j % (X // 2)]
                nc.gpsimd.tensor_scalar(f, f, SX, None, ALU.mult).then_inc(s_el, 1)
                pool.wait_ge(s_el, 2 * j + 1)
                nc.gpsimd.tensor_tensor(e_lo[:, j], f, e_hi[:, j], ALU.subtract).then_inc(s_el, 1)
            pool.wait_ge(s_el, 2 * X)
            nc.gpsimd.memset(big[:, half:half + (AHEAD + 4) * E], 0.0).then_inc(s_zero, 1)
            nc.gpsimd.memset(idx_s[:, :], int(EMPTY)).then_inc(s_zero, 1)
            pool.wait_ge(s_zero, 2)

            pool.wait_ge(s_place, 1)
            nc.gpsimd.memset(et_f[:, 0], 0.0).then_inc(s_et, 1)
            for j in range(1, X):
                nc.gpsimd.tensor_scalar(et_c[:, :], iota_t[:, :], start[:, j:j + 1], None, ALU.is_ge).then_inc(s_et, 1)
                pool.wait_ge(s_et, 2 * j)
                nc.gpsimd.tensor_tensor(et_f[:, j % 2], et_f[:, (j + 1) % 2], et_c[:, :], ALU.add).then_inc(s_et, 1)
                pool.wait_ge(s_et, 2 * j + 1)
            nc.gpsimd.tensor_copy(et_i[:, :], et_f[:, (X - 1) % 2]).then_inc(s_table, 1)
            for b in range(B):
                ins = nc.gpsimd.tensor_scalar(oh_t[:, b], iota_t[:, :], dest[:, b:b + 1], scale_s[:, :],
                                              ALU.is_equal, ALU.mult)
            ins.then_inc(s_dest, 1)

            rows = out.rearrange("b n e -> (b n) e")

            def scatter(i):
                pool.indirect_dma_start(rows, bass.IndirectOffsetOnAxis(ap=idx_s[:, i:i + 1], axis=0), yo[:, i], None,
                                        bounds_check=B * N - 1, oob_is_err=False).then_inc(s_sc[i], 16)

            for i in range(4):
                scatter(i)
            for i in range(2):
                pool.wait_ge(s_st[i], NG // 2 * 16)
            pool.wait_ge(s_table, 3)
            nq = pool.value_load(nq_i[0:1, 0:1], min_val=1, max_val=TILES // 4)

            def gather(j):
                pool.indirect_dma_start(xg[:, j], None, rows,
                                        bass.IndirectOffsetOnAxis(ap=idx_g[:, j:j + 1], axis=0),
                                        bounds_check=B * N - 1, oob_is_err=False).then_inc(s_ga[j], 16)

            def row_rstd(i, n):
                pool.wait_ge(s_fvar, n + 1)
                pool.nop(nofuse=True)
                nc.gpsimd.tensor_tensor(rstd[:, i:i + 1], vpe[:, i:i + 1], mhalf[:, 0:1], ALU.pow).then_inc(s_frs, 1)

            pool.wait_ge(s_idx, 1)
            for j in range(4):
                gather(j)
            for j in range(4):
                row_rstd(j, j)
                gather(4 + j)
            with pool.Fori(0, TILES // (AHEAD * RB)) as block_of_rounds:
                with pool.If(block_of_rounds * (2 * RB) < nq):
                    with pool.Fori(0, RB) as r_in_block:
                        r = block_of_rounds * RB + r_in_block
                        for h in range(2):
                            with pool.If(r * 2 + h < nq):
                                for i in range(4):
                                    n = r * AHEAD + h * 4 + i
                                    row_rstd(i, n + 4)
                                    pool.wait_ge(s_fin, n + 3)
                                    pool.nop(nofuse=True)
                                    pool.wait_ge(s_idx, n + 2)
                                    pool.nop(nofuse=True)
                                    scatter(i)
                                    gather(h * 4 + i)
                            with pool.Else():
                                pool.nop()
                            pool.nop()
                with pool.Else():
                    pool.nop()
                pool.nop()
            for i in range(4):
                pool.wait_ge(s_sc[i], nq * 16 + 16)
                pool.nop(nofuse=True)
            for j in range(AHEAD):
                pool.wait_ge(s_ga[j], (nq + (1 - j // 4)) // 2 * 16 + 16)
                pool.nop(nofuse=True)

        @block.scalar
        def _(act):
            for h in range(2):
                act.wait_ge(s_setup_pe, h + 1)
                for c in range(2):
                    ins = nc.scalar.activation(w_hi[:, 2 * h + c, 0:3 * D], bank[h][:, c * 3 * D:(c + 1) * 3 * D],
                                               ACT.Copy, scale=SW)
                ins.then_inc(s_setup_a, 1)
            nc.scalar.activation(w_hi[:, :, 3 * D:NC], gw, ACT.Copy, scale=SGATE).then_inc(s_setup_a, 1)
            act.wait_ge(s_setup_pe, 3)
            nc.scalar.activation(woT[:, 0:E], bank[2][:, :], ACT.Copy).then_inc(s_setup_a, 1)
            act.wait_ge(s_setup_pe, 5)
            nc.scalar.activation(woT[:, E:E + X], bank[4][:, 0:X], ACT.Copy).then_inc(s_setup_a, 1)

            def energy(step):
                act.wait_ge(s_g, step)
                nc.scalar.activation(g_hi[:, 0:E], p_out[0][:, :], ACT.Copy, scale=OUT_SCALE / (SQ * SQ))
                nc.scalar.activation(g_hi[:, E:E + X], p_out[1][:, 0:X], ACT.Copy,
                                     scale=OUT_SCALE * SLOG / (SQ * SQ)).then_inc(s_gh, 1)

            def y(n, L, i, h):
                if i == 0:
                    act.wait_ge(s_rs, L + 1)
                    act.nop(nofuse=True)
                nc.scalar.activation(y0[:, i], xr[:, L % RING, i], ACT.Identity, bias=nmr[:, h, i:i + 1],
                                     scale=rs[:, h, i:i + 1]).then_inc(s_y, 1)

            def high(n, i):
                act.wait_ge(s_T, n + 1)
                nc.scalar.activation(y_hi[:, i], p_xT[i % 2][:, :], ACT.Copy).then_inc(s_hi, 1)

            def body(L, h, a1, a2, first=False):
                k = L * GT
                M = L - GB
                m = M * GT

                def square(i):
                    if a2:
                        if i == 0:
                            act.wait_ge(s_r1, M + 1)
                        act.wait_ge(s_nm1, M * 2 + i // 2 + 1)
                        act.nop(nofuse=True)
                        nc.scalar.activation(squares[:, i], xr[:, M % RING, i], ACT.Square, bias=nmean1[:, i:i + 1],
                                             accum_out=ssq1[:, i:i + 1]).then_inc(s_sq, 1)

                def qkv_high(i):
                    act.wait_ge(s_qkv, k + i + 1)
                    nc.scalar.activation(qkv[:, i, :, 0, :], p_qkv[i % 2][:, 0:3 * D].rearrange("p (m d) -> p m d", m=3),
                                         ACT.Copy, scale=SQ / (SY * SW)).then_inc(s_qh, 1)

                def copy_qT(i):
                    act.wait_ge(s_qt, k + i + 1)
                    act.nop(nofuse=True)
                    nc.scalar.activation(qT[:, L % RING, i], p_qT16, ACT.Copy).then_inc(s_qc, 1)

                for i in range(GT):
                    if a1:
                        if i > 0:
                            copy_qT(i - 1)
                        qkv_high(i)
                        if not (first and i == 0):
                            high(k + i + 2, (i + 2) % GT)
                            y(k + i + 3, L + (i + 3) // GT, (i + 3) % GT, (h + (i + 3) // GT) % 2)
                    if i > 0:
                        square(i - 1)
                square(GT - 1)
                if a1:
                    copy_qT(GT - 1)

            act.sem_inc(s_sq, GT)
            for i in range(3):
                y(i, 0, i, 0)
            high(0, 0)
            high(1, 1)
            with act.Fori(0, GB // 2) as g:
                for h in range(2):
                    body(g * 2 + h, h, True, False)
            with act.Fori(1, B) as step:
                high(step * TB + 2, 2)
                y(step * TB + 3, step * GB, 3, 0)
                energy(step)
                for h in range(2):
                    body(step * GB + h, h, True, True, first=h == 0)
                with act.Fori(1, GB // 2) as g:
                    for h in range(2):
                        body(step * GB + g * 2 + h, h, True, True)
            energy(B)
            with act.Fori(0, GB) as g:
                body(g + B * GB, 0, False, True)

            for j in range(X):
                act.wait_ge(s_ex, 16 if j < X // 2 else 32)
                nc.scalar.activation(e_hi[:, j], e_f[:, j % (X // 2)], ACT.Copy, scale=SX).then_inc(s_eh, 1)

            act.wait_ge(s_gates, 1)
            for q in range(4):
                for h in range(2):
                    t = slice(q * HT // 4, (q + 1) * HT // 4)
                    ins = nc.scalar.activation(g_order[:, t, h], g_halves[:, h, t], ACT.Copy)
                ins.then_inc(s_go, 1)
            for q in range(4):
                act.wait_ge(s_gt, q + 1)
                w = HT * P // 4
                nc.scalar.activation(gT[:, q * w:(q + 1) * w], bank[1 + q][0:2 * BX, 0:w], ACT.Copy).then_inc(s_gc, 1)
            with act.Fori(0, B) as b:
                for h in range(2):
                    act.wait_ge(s_eq, b * 2 + h + 1)
                    act.wait_ge(s_list, b * 2 + h + 1)
                    act.nop(nofuse=True)
                    nc.scalar.activation(oh_w[:, h, 0], eq_w[:, h], ACT.Copy, scale=tok_a[:, bass.ds(b, 1)]).then_inc(s_ea, 1)
                act.wait_ge(s_list, b * 2 + 4)
                act.nop(nofuse=True)
                nc.scalar.activation(win_list[0:2 * WX, bass.ds(b, 1)], bank[1][0:2 * WX, 0:P], ACT.Copy).then_inc(s_wl, 1)

            act.wait_ge(s_table, 3)
            nq = act.value_load(nq_i[0:1, 0:1], min_val=1, max_val=TILES // 4)

            def row_high(i, n):
                act.wait_ge(s_fT, n + 1)
                nc.scalar.activation(y_hi[:, i], p_xT[i % 2][:, :], ACT.Copy).then_inc(s_fhi, 1)

            nc.scalar.activation(idx_g[:, :], table[:, 0:AHEAD], ACT.Copy).then_inc(s_idx, 1)
            row_high(0, 0)
            row_high(1, 1)
            with act.Fori(0, TILES // (AHEAD * RB)) as block_of_rounds:
                with act.If(block_of_rounds * (2 * RB) < nq):
                    with act.Fori(0, RB) as r_in_block:
                        r = block_of_rounds * RB + r_in_block
                        for h in range(2):
                            with act.If(r * 2 + h < nq):
                                for i in range(4):
                                    n = r * AHEAD + h * 4 + i
                                    j = h * 4 + i
                                    act.wait_ge(s_ga[j], r * 16 + 16)
                                    act.wait_ge(s_sc[i], (r * 2 + h + 1) * 16)
                                    act.nop(nofuse=True)
                                    nc.scalar.activation(idx_g[:, j:j + 1], table[:, bass.ds(n + AHEAD, 1)], ACT.Copy)
                                    nc.scalar.activation(idx_s[:, i:i + 1], table[:, bass.ds(n, 1)], ACT.Copy).then_inc(s_idx, 1)
                                    row_high((i + 2) % 4, n + 2)
                            with act.Else():
                                act.nop()
                            act.nop()
                with act.Else():
                    act.nop()
                act.nop()

        @block.vector
        def _(dve):
            for h in range(2):
                dve.wait_ge(s_setup_a, h + 1)
                for c in range(2):
                    ins = nc.vector.scalar_tensor_tensor(
                        w_lo[:, 2 * h + c, 0:3 * D], bank[h][:, c * 3 * D:(c + 1) * 3 * D], SW,
                        w_hi[:, 2 * h + c, 0:3 * D], ALU.mult, ALU.subtract)
                ins.then_inc(s_setup_v, 1)
            dve.wait_ge(s_setup_a, 3)
            nc.vector.scalar_tensor_tensor(w_lo[:, :, 3 * D:NC], gw, SGATE, w_hi[:, :, 3 * D:NC],
                                           ALU.mult, ALU.subtract)
            dve.wait_ge(s_setup_pe, 4)
            nc.vector.tensor_tensor(gwc, gw, bank[3][:, 0:X].unsqueeze(1).to_broadcast([P, CH, X]),
                                    ALU.subtract).then_inc(s_setup_v, 1)

            def x_stats(L, i, h):
                nc.vector.bn_stats(stats[:, h, i], xr[:, L % RING, i]).then_inc(s_bn, 1)

            def stats_ready(L, h):
                dve.wait_ge(s_ld[h], (L // 2 + 2) * 16)
                dve.wait_ge(s_rs, L + 1)
                dve.nop(nofuse=True)

            def x_moments(L, h):
                for i in range(GT):
                    dve.wait_ge(s_bn, L * GT + i + 1)
                    dve.nop(nofuse=True)
                    nc.vector.bn_aggr(mv[:, h, i], stats[:, h, i]).then_inc(s_mv, 1)

            def rest(n, i):
                dve.wait_ge(s_hi, n + 1)
                nc.vector.tensor_tensor(y_lo[:, i], p_xT[i % 2][:, :], y_hi[:, i], ALU.subtract).then_inc(s_lo, 1)

            def energy(step):
                dve.wait_ge(s_en, step)
                nc.vector.tensor_copy(en_half[:, :], p_en[:, 0:D]).then_inc(s_half, 1)
                dve.wait_ge(s_half, step)
                nc.vector.tensor_tensor(en[:, :, :], p_en[:, D:2 * D].unsqueeze(1).to_broadcast([P, 2, D]),
                                        en_half[:, :].unsqueeze(1).to_broadcast([P, 2, D]), ALU.add).then_inc(s_ec, 1)

            def g_rest(step):
                dve.wait_ge(s_gh, step)
                nc.vector.scalar_tensor_tensor(g_lo[:, 0:E], p_out[0][:, :], OUT_SCALE / (SQ * SQ), g_hi[:, 0:E],
                                               ALU.mult, ALU.subtract)
                nc.vector.scalar_tensor_tensor(g_lo[:, E:E + X], p_out[1][:, 0:X], OUT_SCALE * SLOG / (SQ * SQ),
                                               g_hi[:, E:E + X], ALU.mult, ALU.subtract).then_inc(s_gl, 1)

            def body(L, h, a1, a2, first=False):
                k = L * GT
                M = L - GB
                m = M * GT

                def qkv_rest(i):
                    if a1:
                        dve.wait_ge(s_qh, k + i + 1)
                        nc.vector.scalar_tensor_tensor(
                            qkv[:, i, :, 1, :], p_qkv[i % 2][:, 0:3 * D].rearrange("p (m d) -> p m d", m=3),
                            SQ / (SY * SW), qkv[:, i, :, 0, :], ALU.mult, ALU.subtract)
                        w = slice(0, 2 * X if a2 else X)
                    else:
                        dve.wait_ge(s_qkv, k + i + 1)
                        dve.nop(nofuse=True)
                        w = slice(X, 2 * X)
                    nc.vector.tensor_copy(lg[:, k + i, w], p_qkv[i % 2][:, 3 * D + w.start:3 * D + w.stop]).then_inc(s_ql, 1)

                def add(i):
                    if a2:
                        dve.wait_ge(s_sq, m + i + 1)
                        dve.nop(nofuse=True)
                        dve.wait_ge(s_o, m + i + 1)
                        nc.vector.scalar_tensor_tensor(xr[:, M % RING, i], p_out[i % 2][:, :], 1.0 / SQ,
                                                       xr[:, M % RING, i], ALU.mult, ALU.add,
                                                       accum_out=sum1[:, i:i + 1]).then_inc(s_x1, 1)

                def means(i):
                    if a2:
                        dve.wait_ge(s_x1, m + i + 3)
                        nc.vector.tensor_scalar(nmean1[:, i - 1:i + 1], sum1[:, i - 1:i + 1], -1.0 / E, None,
                                                ALU.mult).then_inc(s_nm1, 1)

                for i in range(GT):
                    add(i)
                    if a1 and i == 0 and not first:
                        stats_ready(L, h)
                    if a1 and i < 2 and not first:
                        x_stats(L + 2, 2 * i, h)
                        if i == 0:
                            x_stats(L + 2, 1, h)
                    qkv_rest(i)
                    if i % 2 == 1:
                        means(i)
                    if a1:
                        if i == 1 and not first:
                            x_stats(L + 2, 3, h)
                        if not (first and i == 0):
                            rest(k + i + 2, (i + 2) % GT)
                        if i == 2:
                            x_moments(L + 2, h)

            for h in range(2):
                dve.wait_ge(s_ld[h], 16)
                for i in range(GT):
                    x_stats(h, i, h)
                x_moments(h, h)
            rest(0, 0)
            rest(1, 1)
            with dve.Fori(0, GB // 2) as g:
                for h in range(2):
                    body(g * 2 + h, h, True, False)
            with dve.Fori(1, B) as step:
                energy(step)
                stats_ready(step * GB, 0)
                for i in range(GT):
                    x_stats(step * GB + 2, i, 0)
                rest(step * TB + 2, 2)
                g_rest(step)
                for h in range(2):
                    body(step * GB + h, h, True, True, first=h == 0)
                with dve.Fori(1, GB // 2) as g:
                    for h in range(2):
                        body(step * GB + g * 2 + h, h, True, True)
            energy(B)
            g_rest(B)
            with dve.Fori(0, GB) as g:
                body(g + B * GB, 0, False, True)

            chain = Chain(dve, s_dve)
            V = nc.vector
            A, Bw, Cw = work_a[:, :], work_b, work_c
            G = gates[:, :]

            def tiles(a):
                return a.rearrange("p (k j) -> p k j", j=X)

            def rows_(a):
                return a.unsqueeze(2).to_broadcast([P, K, X])

            def sums(a):
                return V.tensor_reduce(part[:, :].rearrange("p (b j) -> p b j", b=B),
                                       a.rearrange("p (b t j) -> p b j t", b=B, j=X), AX.X, ALU.add)

            total = bank[0][:, 0:BX]

            dve.wait_ge(s_sd, NG + 2)
            chain(V.tensor_tensor(tiles(A), lg[:, 0:K, 0:X], rows_(sd0[:, 0:K]), ALU.mult))
            chain(V.scalar_tensor_tensor(tiles(A), lg[:, TB:TB + K, X:2 * X], SGATE / (SQ * SLOG), tiles(A),
                                         ALU.mult, ALU.add))
            dve.wait_ge(s_r1, NG + 1)
            chain(V.tensor_tensor(tiles(A), tiles(A), rows_(r1[:, :]), ALU.mult))
            chain(V.tensor_scalar(G, A, 1.0 / SGATE, CLIP_EPS, ALU.mult, ALU.max))

            with dve.Fori(0, ROUNDS // SB) as r:
                n0 = chain.n
                for i in range(SB):
                    sums(G).then_inc(s_part, 1)
                    dve.wait_ge(s_sum, r * SB + i + 1)
                    chain(V.reciprocal(inv[:, :], total), r * 5 * SB)
                    chain(V.tensor_tensor(by_tile(G), by_tile(G), to_tiles(inv[:, :]), ALU.mult), r * 5 * SB)
                    chain(V.tensor_reduce(row[:, :], tiles(G), AX.X, ALU.add), r * 5 * SB)
                    chain(V.reciprocal(row_r[:, :], row[:, :]), r * 5 * SB)
                    chain(V.tensor_tensor(tiles(G), tiles(G), rows_(row_r[:, :]), ALU.mult), r * 5 * SB)
                assert chain.n - n0 == 5 * SB
            chain.n += (ROUNDS // SB - 1) * 5 * SB
            V.engine_nop().then_inc(s_gates, 1)

            dve.wait_ge(s_const2, 4)
            T2 = 2 * BX
            junk = qT_w[0:T2, KX:KX + HT * P // 2].bitcast(F16)
            c_f = cand[0:T2].bitcast(F32)
            total1 = bank[5][0:T2, 0:1]
            chain(V.tensor_copy(cand[:, :], bits_i[:, 0:1]))
            chain(V.tensor_tensor(mask[:, :], mask_a[:, :], mask_b[:, :], ALU.add))
            chain(V.scalar_tensor_tensor(win_f[:, :], mask_b[:, :], -float(WX), win_f[:, :], ALU.mult, ALU.add))
            chain(V.tensor_tensor(win_f[:, :], win_f[:, :], mask[:, :], ALU.mult))
            chain(V.tensor_reduce(win_s[:, :], win_f[:, :], AX.X, ALU.add))
            chain(V.scalar_tensor_tensor(mask_b[:, :], mask_a[:, :], float(TB), mask_b[:, :], ALU.mult, ALU.add))
            chain(V.tensor_reduce(scale_s[:, :], mask_b[:, :], AX.X, ALU.add))
            dve.wait_ge(s_gc, 4)
            with dve.Fori(0, BITS // BB) as r:
                n0 = chain.n
                for i in range(BB):
                    V.tensor_scalar(junk, gT, c_f, -(CAP - 0.5) / 2, ALU.is_ge, ALU.add, accum_out=cnt[0:T2]).then_inc(s_cnt, 1)
                    b0, b1 = bass.ds(r * BB + i, 1), bass.ds(r * BB + i + 1, 1)
                    V.tensor_tensor(cand_up[:, :], cand[:, :], bits_i[:, b1], ALU.bitwise_or)
                    chain(V.tensor_tensor(cand_down[:, :], cand[:, :], bits_2[:, b0], ALU.bitwise_xor), r * 2 * BB)
                    dve.wait_ge(s_tot, r * BB + i + 1)
                    dve.nop(nofuse=True)
                    chain(V.tensor_scalar(c_f, total1, cand_up[0:T2].bitcast(F32), cand_down[0:T2].bitcast(F32),
                                          ALU.min, ALU.max), r * 2 * BB)
                assert chain.n - n0 == 2 * BB
            chain.n += (BITS // BB - 1) * 2 * BB
            V.tensor_scalar(junk, gT, c_f, -CAP / 2, ALU.is_gt, ALU.add, accum_out=cnt[0:T2]).then_inc(s_cnt, 1)
            V.tensor_scalar(spread[0:BX, 0], ones1[0:BX, :], c_f[0:BX], None, ALU.mult)
            dve.wait_ge(s_tot, BITS + 1)
            chain(V.tensor_scalar(need1[0:BX], total1[0:BX], -1.0 / HUGE, None, ALU.mult))
            V.tensor_scalar(spread[0:BX, 1], ones1[0:BX, :], need1[0:BX], None, ALU.mult).then_inc(s_cnt, 1)

            def by_row(a):
                return a.rearrange("p (b t j) -> p b j t", b=B, j=X)

            def rows3(a):
                return a.rearrange("p (b j t) -> p b j t", b=B, j=X)

            def rows2(a):
                return a.rearrange("p (r t) -> p r t", t=TB)

            def of_row(a):
                return a.unsqueeze(2).to_broadcast([P, BX, TB])

            def of_row3(a):
                return a.rearrange("p (b j) -> p b j", b=B).unsqueeze(3).to_broadcast([P, B, X, TB])

            def f16(a):
                b = a.bitcast(F16)
                return b[:, 0:KX], b[:, KX:2 * KX]

            def starts(scan):
                ends = rows2(scan)[:, :, TB - 1]
                V.tensor_copy(prev[:, 1:BX], ends[:, 0:BX - 1])
                chain(V.memset(prev[:, 0:1], 0.0))
                chain(V.tensor_tensor(part[:, :], ends, prev[:, :], ALU.subtract))
                V.engine_nop().then_inc(s_part, 1)

            (above, equal), (prefix, low), (flag, chosen) = f16(Bw), f16(Cw), f16(A)
            for j in range(X):
                V.tensor_scalar(rows3(flag)[:, :, j], by_row(G)[:, :, j], 0.5, 2.0 * (j + 1), ALU.is_gt, ALU.add)
            dve.wait_ge(s_tot, BITS + 2)
            chain(V.tensor_copy(thr_need[:, :, :], bank[5][:, 0:2 * BX].rearrange("p (a r) -> p a r", a=2)))
            chain(V.tensor_tensor(rows3(equal), by_row(G), of_row3(thr_need[:, 0]), ALU.is_equal))
            chain(V.tensor_tensor_scan(prefix, one1[:, :].to_broadcast([P, KX]), equal, 0.0, ALU.mult, ALU.add))
            starts(prefix)
            V.tensor_tensor(rows3(above), by_row(G), of_row3(thr_need[:, 0]), ALU.is_gt)
            chain(V.scalar_tensor_tensor(lim[:, :], prev[:, :], 1.0, thr_need[:, 1], ALU.add, ALU.add))
            dve.wait_ge(s_sum, ROUNDS + 1)
            chain(V.tensor_tensor(lim[:, :], lim[:, :], total, ALU.subtract))
            chain(V.tensor_tensor(rows2(low), rows2(prefix), of_row(lim[:, :]), ALU.is_lt))
            chain(V.tensor_tensor(low, low, equal, ALU.mult))
            chain(V.tensor_tensor(chosen, above, low, ALU.add))

            chain(V.tensor_tensor(chosen, chosen, flag, ALU.mult))
            chain(V.tensor_reduce(m_max[:, :].rearrange("p (b t) -> p b t", b=B),
                                  chosen.rearrange("p (b j t) -> p b t j", b=B, j=X), AX.X, ALU.max))
            active, prefix = f16(Bw)
            for j in range(X):
                ins = V.tensor_scalar(rows3(active)[:, :, j], m_max[:, :].rearrange("p (b t) -> p b t", b=B),
                                      2.0 * (j + 1) + 1.0, None, ALU.is_equal)
            chain(ins)

            chain(V.tensor_tensor_scan(prefix, one1[:, :].to_broadcast([P, KX]), active, 0.0, ALU.mult, ALU.add))
            starts(prefix)
            dve.wait_ge(s_sum, ROUNDS + 2)
            counts = bank[0][:, BX:2 * BX].rearrange("p (b j) -> p j b", b=B)

            def xb(a):
                return a[:, :].rearrange("p (j b) -> p j b", j=X)

            V.tensor_reduce(tot[:, :], counts, AX.X, ALU.add)
            chain(V.tensor_copy(xb(sel), counts))
            chain(V.tensor_tensor_scan(excl[:, :], one1[:, :].to_broadcast([P, BX]), sel[:, :], 0.0, ALU.mult, ALU.add))
            chain(V.tensor_tensor(excl[:, :], excl[:, :], sel[:, :], ALU.subtract))
            chain(V.tensor_scalar(nt_i[:, :], tot[:, :], P - 1.0, None, ALU.add))
            chain(V.tensor_single_scalar(nt_i[:, :], nt_i[:, :], 7, ALU.arith_shift_right))
            chain(V.tensor_copy(nt_f[:, :], nt_i[:, :]))
            chain(V.tensor_tensor_scan(cum[:, :], one1[:, :].to_broadcast([P, X]), nt_f[:, :], 0.0, ALU.mult, ALU.add))
            chain(V.tensor_tensor(start[:, :], cum[:, :], nt_f[:, :], ALU.subtract))
            chain(V.tensor_scalar(nq_i[:, :], cum[:, X - 1:X], 1.0, 3.0, ALU.max, ALU.add))
            V.tensor_single_scalar(nq_i[:, :], nq_i[:, :], 2, ALU.arith_shift_right).then_inc(s_table, 1)
            chain(V.scalar_tensor_tensor(corr[:, :], start[:, :], float(P), xb(excl)[:, :, 0], ALU.mult, ALU.subtract))
            chain(V.tensor_tensor(xb(base_i), xb(excl), corr[:, :].unsqueeze(2).to_broadcast([P, X, B]), ALU.add))
            V.tensor_single_scalar(tile_i[:, :], base_i[:, :], 7, ALU.arith_shift_right)
            chain(V.tensor_single_scalar(off_i[:, :], base_i[:, :], P - 1, ALU.bitwise_and))
            V.tensor_copy(tile_f[:, :], tile_i[:, :])
            chain(V.tensor_tensor(xb(off_f), xb(off_i), win_x[:, :].unsqueeze(2).to_broadcast([P, X, B]), ALU.add))
            chain(V.tensor_tensor(lim[:, :], bank[0][:, 0:BX], prev[:, :], ALU.subtract))
            chain(V.tensor_tensor(lim[:, :].rearrange("p (b j) -> p j b", b=B), lim[:, :].rearrange("p (b j) -> p j b", b=B),
                                  xb(off_f), ALU.add))
            chain(V.tensor_tensor(xb(sel), xb(tile_f), mask[:, :].unsqueeze(2).to_broadcast([P, X, B]), ALU.mult))
            chain(V.tensor_reduce(dest[:, :], sel[:, :].rearrange("p (j b) -> p b j", j=X), AX.X, ALU.add))
            V.tensor_scalar(dest[:, :], dest[:, :], win_s[:, :], None, ALU.add).then_inc(s_place, 1)
            places = A
            chain(V.tensor_tensor(rows2(places), rows2(prefix), of_row(lim[:, :]), ALU.add))
            chain(V.tensor_tensor(places, places, active, ALU.mult))
            chain(V.tensor_reduce(row[:, :].rearrange("p (b t) -> p b t", b=B),
                                  places.rearrange("p (b j t) -> p b t j", b=B, j=X), AX.X, ALU.add))
            chain(V.tensor_scalar(pos_i[:, :], row[:, :], -1.0, None, ALU.add))
            V.tensor_single_scalar(lo_i[:, :], pos_i[:, :], P - 1, ALU.bitwise_and)
            chain(V.tensor_single_scalar(hi_i[:, :], pos_i[:, :], 7, ALU.arith_shift_right))
            V.tensor_copy(lo16[:, :], lo_i[:, :])
            chain(V.tensor_copy(hi16[:, :], hi_i[:, :]))

            dve.wait_ge(s_const2, 5)
            dve.sem_inc(s_list, 2)
            with dve.Fori(0, B) as b:
                for h in range(2):
                    n0 = chain.n
                    tiles_h = bass.ds((b * 2 + h) * HT, HT)
                    dve.wait_ge(s_list, b * 2 + h + 1)
                    dve.nop(nofuse=True)
                    V.tensor_tensor(eq_w[:, h], iota_c[:, :, :], hi16[:, tiles_h].unsqueeze(1).to_broadcast([P, WX, HT]),
                                    ALU.is_equal).then_inc(s_eq, 1)
                    V.tensor_tensor(oh_l[:, h], iota_l, lo16[:, tiles_h].unsqueeze(1).to_broadcast([P, P, HT]), ALU.is_equal)
                    dve.wait_ge(s_eq, b * 2 + h + 1)
                    V.tensor_tensor(oh_w[:, h, 1], eq_w[:, h], tok_b[:, h * HT:(h + 1) * HT].unsqueeze(1).to_broadcast([P, WX, HT]),
                                    ALU.mult).then_inc(s_oh, 1)

            dve.wait_ge(s_tab, 1)
            chain(V.tensor_scalar(empty[:, :], bank[2][:, 0:TABLE], 0.0, EMPTY + 1.0, ALU.is_equal, ALU.mult))
            V.scalar_tensor_tensor(table[:, :], bank[2][:, 0:TABLE], -1.0, empty[:, :], ALU.add, ALU.add).then_inc(s_table, 1)

            dve.wait_ge(s_table, 3)
            nq = dve.value_load(nq_i[0:1, 0:1], min_val=1, max_val=TILES // 4)

            def row_stats(n, j, r):
                i = j % 4
                dve.wait_ge(s_ga[j], r * 16 + 16)
                dve.nop(nofuse=True)
                V.bn_stats(stats[:, 0, i], xg[:, j]).then_inc(s_fbn, 1)
                dve.wait_ge(s_fbn, n + 1)
                dve.nop(nofuse=True)
                V.bn_aggr(mv[:, 0, i], stats[:, 0, i]).then_inc(s_fmv, 1)

            def row_var(n, i):
                dve.wait_ge(s_fmv, n + 1)
                V.tensor_scalar(vpe[:, i:i + 1], mv[:, 0, i, 1:2], LN_EPS, SY ** -2, ALU.add, ALU.mult).then_inc(s_fvar, 1)

            def row_y(n, j):
                i = j % 4
                dve.wait_ge(s_frs, n + 1)
                V.tensor_scalar(y0[:, i], xg[:, j], mv[:, 0, i, 0:1], rstd[:, i:i + 1], ALU.subtract, ALU.mult).then_inc(s_fy, 1)

            def row_rest(i, n):
                dve.wait_ge(s_fhi, n + 1)
                V.tensor_tensor(y_lo[:, i], p_xT[i % 2][:, :], y_hi[:, i], ALU.subtract).then_inc(s_flo, 1)

            for i in range(4):
                row_stats(i, i, 0)
                row_var(i, i)
                if i > 0:
                    row_y(i - 1, i - 1)
                if i > 1:
                    row_rest(i - 2, i - 2)
            with dve.Fori(0, TILES // (AHEAD * RB)) as block_of_rounds:
                with dve.If(block_of_rounds * (2 * RB) < nq):
                    with dve.Fori(0, RB) as r_in_block:
                        r = block_of_rounds * RB + r_in_block
                        for h in range(2):
                            with dve.If(r * 2 + h < nq):
                                for i in range(4):
                                    n = r * AHEAD + h * 4 + i
                                    row_stats(n + 4, (h * 4 + i + 4) % AHEAD, r + h)
                                    row_y(n + 3, (h * 4 + i + 3) % AHEAD)
                                    row_var(n + 4, i)
                                    row_rest((i + 2) % 4, n + 2)
                                    dve.wait_ge(s_sc[i], (r * 2 + h + 1) * 16)
                                    dve.wait_ge(s_fmm, n + 1)
                                    V.scalar_tensor_tensor(yo[:, i], p_out[i % 2][:, :], 1.0 / (SY * SX), xg[:, h * 4 + i],
                                                           ALU.mult, ALU.add).then_inc(s_fin, 1)
                            with dve.Else():
                                dve.nop()
                            dve.nop()
                with dve.Else():
                    dve.nop()
                dve.nop()

        @block.tensor
        def _(pe):
            pe.sem_inc(s_lo, 2)
            pe.sem_inc(s_ql, 2)
            pe.sem_inc(s_qc, 1)
            pe.sem_inc(s_x1, 2)
            pe.sem_inc(s_fin, 2)
            pe.wait_ge(s_const, 2)
            pe.wait_ge(s_w, 16 * 6)
            for h in range(2):
                for c in range(2):
                    for m in range(3):
                        ins = nc.tensor.transpose(bank[h][:, c * 3 * D + m * D:c * 3 * D + (m + 1) * D],
                                                  wall[:, m, (2 * h + c) * P:(2 * h + c + 1) * P], ident[0:D, 0:D])
                ins.then_inc(s_setup_pe, 1)
            for c in range(CH):
                ins = nc.tensor.transpose(bank[2][:, c * P:(c + 1) * P], wod[:, c].rearrange("p r d -> p (r d)"),
                                          ident[:, :])
            ins.then_inc(s_setup_pe, 1)
            for c in range(CH):
                ins = nc.tensor.matmul(bank[3][:, 0:X], inv_e[:, :], gw[:, c], start=c == 0, stop=c == CH - 1)
            ins.then_inc(s_setup_pe, 1)
            pe.wait_ge(s_setup_v, 3)
            for c in range(CH):
                ins = nc.tensor.matmul(bank[4][:, 0:X], wod[:, c].rearrange("p r d -> p (r d)"), gwc[:, c],
                                       start=c == 0, stop=c == CH - 1)
            ins.then_inc(s_setup_pe, 1)
            pe.wait_ge(s_setup_a, 5)

            def zero_energy(start):
                return nc.tensor.matmul(p_en[:, 0:P], zero16[:, :], zero16[:, :], start=start, stop=not start)

            def g_product(step):
                pe.wait_ge(s_ec, step)
                pe.wait_ge(s_x1, (step - 1) * TB + 2)
                en_w = en[:, :, :].rearrange("p r d -> p (r d)")
                nc.tensor.matmul(p_out[0][:, :], en_w, woT[:, 0:E], start=True, stop=True)
                nc.tensor.matmul(p_out[1][:, 0:X], en_w, woT[:, E:E + X], start=True, stop=True).then_inc(s_g, 1)

            def transpose(n, i):
                pe.wait_ge(s_y, n + 1)
                for c in range(CH):
                    ins = nc.tensor.transpose(p_xT[i % 2][:, c * P:(c + 1) * P], y0[:, i, c * P:(c + 1) * P],
                                              ident[:, :])
                ins.then_inc(s_T, 1)

            def attend(M, i):
                pe.wait_ge(s_x1, M * GT + i + 1)
                pe.nop(nofuse=True)
                for g, start in ((g_hi, True), (g_lo, False)):
                    ins = nc.tensor.matmul(p_out[i % 2][:, :], qT[:, M % RING, i], g[:, 0:E], start=start, stop=not start)
                ins.then_inc(s_o, 1)

            def project(k, i):
                pe.wait_ge(s_ql, k + i + 1)
                pe.nop(nofuse=True)
                pe.wait_ge(s_lo, k + i + 3)
                for c in range(CH):
                    f = slice(c * P, (c + 1) * P)
                    nc.tensor.matmul(p_qkv[i % 2][:, 0:NC], y_hi[:, i, f], w_hi[:, c], start=c == 0, stop=False)
                    nc.tensor.matmul(p_qkv[i % 2][:, 0:NC], y_hi[:, i, f], w_lo[:, c], start=False, stop=False)
                    ins = nc.tensor.matmul(p_qkv[i % 2][:, 0:NC], y_lo[:, i, f], w_hi[:, c], start=False, stop=c == CH - 1)
                return ins

            def body(L, a1, a2, first=False, last=False):
                k = L * GT
                M = L - GB

                def energy_and_qT(i):
                    if a1:
                        pe.wait_ge(s_ql, k + i + 3)
                        pe.wait_ge(s_qc, k + i + 1)
                        nc.tensor.transpose(p_qT16, qkv[:, i, 0].rearrange("p a d -> p (a d)"), ident16[:, :])
                        nc.tensor.matmul(p_en[:, 0:P], qkv[:, i, 2].rearrange("p a d -> p (a d)"),
                                         qkv[:, i, 1].rearrange("p a d -> p (a d)"), start=False,
                                         stop=False).then_inc(s_qt, 1)

                for i in range(GT):
                    if a1 and not (first and i < 2):
                        ins = project(k, i)
                    if not a1:
                        pe.wait_ge(s_ql, k + i + 1)
                        pe.nop(nofuse=True)
                    if a2:
                        for g, start in ((g_hi, True), (g_lo, False)):
                            ins = nc.tensor.matmul(p_qkv[i % 2][:, NC:NC + X], qT[:, M % RING, i], g[:, E:E + X],
                                                   start=start, stop=not start)
                    ins.then_inc(s_qkv, 1)
                    if a2 and not (last and i == GT - 1):
                        attend(M + (i + 1) // GT, (i + 1) % GT)
                    if i > 0:
                        energy_and_qT(i - 1)
                    if a1 and not (first and i == 0):
                        transpose(k + i + 2, (i + 2) % GT)
                energy_and_qT(GT - 1)

            transpose(0, 0)
            transpose(1, 1)
            zero_energy(True)
            with pe.Fori(0, GB) as g:
                body(g, True, False)
            zero_energy(False).then_inc(s_en, 1)
            with pe.Fori(1, B) as step:
                pe.wait_ge(s_lo, step * TB + 3)
                pe.nop(nofuse=True)
                transpose(step * TB + 2, 2)
                g_product(step)
                for i in range(2):
                    project(step * TB, i)
                pe.wait_ge(s_gl, step)
                zero_energy(True)
                attend(step * GB - GB, 0)
                for h in range(2):
                    body(step * GB + h, True, True, first=h == 0)
                with pe.Fori(1, GB // 2 - 1) as g:
                    for h in range(2):
                        body(step * GB + g * 2 + h, True, True)
                for h in range(2):
                    body(step * GB + GB - 2 + h, True, True, last=h == 1)
                zero_energy(False).then_inc(s_en, 1)
            g_product(B)
            pe.wait_ge(s_gl, B)
            attend(NG - GB, 0)
            with pe.Fori(0, GB - 1) as g:
                body(g + B * GB, False, True)
            body(B * GB + GB - 1, False, True, last=True)

            with pe.Fori(0, ROUNDS) as r:
                pe.wait_ge(s_part, r + 1)
                nc.tensor.matmul(bank[0][:, 0:BX], ones1[:, :], part[:, :], start=True, stop=True).then_inc(s_sum, 1)
            for t in range(HT):
                q, c = t // (HT // 4), t % (HT // 4)
                if c == 0:
                    pe.wait_ge(s_go, q + 1)
                ins = nc.tensor.transpose(bank[1 + q][0:2 * BX, c * P:(c + 1) * P],
                                          g_order[:, t].rearrange("p h b j -> p (h b j)"), ident[:, :])
                if c == HT // 4 - 1:
                    ins.then_inc(s_gt, 1)
            T2 = 2 * BX
            with pe.Fori(0, BITS + 1) as r:
                pe.wait_ge(s_cnt, r + 1)
                pe.nop(nofuse=True)
                nc.tensor.matmul(bank[5][0:T2, 0:1], pair[0:T2, 0:T2], cnt[0:T2], start=True, stop=True).then_inc(s_tot, 1)
            pe.wait_ge(s_cnt, BITS + 2)
            for a in range(2):
                ins = nc.tensor.transpose(bank[5][:, a * BX:(a + 1) * BX], spread[0:BX, a], ident[0:BX, 0:BX])
            ins.then_inc(s_tot, 1)
            pe.wait_ge(s_part, ROUNDS + 1)
            nc.tensor.matmul(bank[0][:, 0:BX], before[:, :], part[:, :], start=True, stop=True).then_inc(s_sum, 1)
            pe.wait_ge(s_part, ROUNDS + 2)
            nc.tensor.matmul(bank[0][:, 0:BX], before[:, :], part[:, :], start=True, stop=True)
            nc.tensor.matmul(bank[0][:, BX:2 * BX], ones1[:, :], part[:, :], start=True, stop=True).then_inc(s_sum, 1)

            pe.sem_inc(s_wl, 1)
            with pe.Fori(0, B) as b:
                pe.wait_ge(s_wl, b + 1)
                for h in range(2):
                    pe.wait_ge(s_oh, b * 2 + h + 1)
                    pe.wait_ge(s_ea, b * 2 + h + 1)
                    for t in range(HT):
                        ins = nc.tensor.matmul(bank[1][0:2 * WX, 0:P], oh_w[:, h, :, :, t].rearrange("p q c -> p (q c)"),
                                               oh_l[:, h, :, t], start=h == 0 and t == 0, stop=h == 1 and t == HT - 1)
                    ins.then_inc(s_list, 1)
            pe.wait_ge(s_dest, 1)
            pe.wait_ge(s_wl, B + 1)
            for b in range(B):
                ins = nc.tensor.matmul(bank[2][:, 0:TABLE], win_list[0:2 * WX, b], oh_t[0:2 * WX, b], start=b == 0,
                                       stop=b == B - 1)
            ins.then_inc(s_tab, 1)

            pe.wait_ge(s_table, 3)
            pe.wait_ge(s_el, 2 * X)
            nq = pe.value_load(nq_i[0:1, 0:1], min_val=1, max_val=TILES // 4)

            def row_transpose(i, n):
                pe.wait_ge(s_fy, n + 1)
                for c in range(CH):
                    ins = nc.tensor.transpose(p_xT[i % 2][:, c * P:(c + 1) * P], y0[:, i, c * P:(c + 1) * P], ident[:, :])
                ins.then_inc(s_fT, 1)

            row_transpose(0, 0)
            row_transpose(1, 1)
            with pe.Fori(0, TILES // (AHEAD * RB)) as block_of_rounds:
                with pe.If(block_of_rounds * (2 * RB) < nq):
                    with pe.Fori(0, RB) as r_in_block:
                        r = block_of_rounds * RB + r_in_block
                        for h in range(2):
                            with pe.If(r * 2 + h < nq):
                                for i in range(4):
                                    n = r * AHEAD + h * 4 + i
                                    j = pe.value_load(et_i[0:1, bass.ts(n, 1)], min_val=0, max_val=X - 1)
                                    pe.wait_ge(s_flo, n + 1)
                                    pe.nop(nofuse=True)
                                    row_transpose((i + 2) % 4, n + 2)
                                    pe.wait_ge(s_fin, n + 1)
                                    for c in range(CH):
                                        f = slice(c * P, (c + 1) * P)
                                        nc.tensor.matmul(p_out[i % 2][:, :], y_hi[:, i, f], e_hi[:, j, c], start=c == 0, stop=False)
                                        nc.tensor.matmul(p_out[i % 2][:, :], y_hi[:, i, f], e_lo[:, j, c], start=False, stop=False)
                                        ins = nc.tensor.matmul(p_out[i % 2][:, :], y_lo[:, i, f], e_hi[:, j, c], start=False,
                                                               stop=c == CH - 1)
                                    ins.then_inc(s_fmm, 1)
                            with pe.Else():
                                pe.nop()
                            pe.nop()
                with pe.Else():
                    pe.nop()
                pe.nop()


_INS = ["L0_attn_x", "L0_attn_wq", "L0_attn_wk", "L0_attn_wv", "L0_attn_wo", "L0_ffn_gate_w", "L0_ffn_experts"]


def kernel(**inputs):
    import numpy as _np
    import concourse.bacc as _bacc
    from concourse import mybir as _mybir
    from concourse.bass_utils import run_bass_kernel_spmd as _run

    nc = _bacc.Bacc("TRN2", target_bir_lowering=False, num_devices=1)
    arrays, args = {}, []
    for name in _INS:
        a = _np.ascontiguousarray(inputs[name])
        arrays[f"in_{name}_dram"] = a
        args.append(nc.dram_tensor(f"in_{name}_dram", a.shape, _mybir.dt.from_np(a.dtype), kind="ExternalInput").ap())
    shape = inputs["L0_attn_x"].shape
    args.append(nc.dram_tensor("out_0_dram", shape, _mybir.dt.float32, kind="ExternalOutput").ap())
    linear_attention_moe_kernel(nc, *args)
    r = _run(nc, [arrays], core_ids=[0])
    return r.results[0]["out_0_dram"]
```
